# Optimizing a Trainium2 kernel written in Bass

```python
import numpy as np
import jax
import jax.numpy as jnp

def _softmax(x, axis=-1):
    return jax.nn.softmax(x, axis=axis)

def _gelu(x):
    return jax.nn.gelu(x, approximate=True)

def _silu(x):
    return jax.nn.silu(x)

def _sigmoid(x):
    return jax.nn.sigmoid(x)

def _layernorm(x, axis=-1, eps=1e-05):
    m = jnp.mean(x, axis=axis, keepdims=True)
    v = jnp.var(x, axis=axis, keepdims=True)
    return (x - m) / jnp.sqrt(v + eps)

def _scatter_add(tgt, idx, src, axis=0):
    return tgt.at[idx].add(src)

def _segment_sum(src, seg, n):
    return jax.ops.segment_sum(src, seg, n)
kernel_name = 'mk_vit_tower_d1_tok_img768_r4_f8819a'

def setup_inputs(seed: int=0):
    np.random.seed(seed)
    _w = jnp.asarray

    def _rec_inputs():
        import jax
        import jax.numpy as jnp
        _rk = jax.random.key(seed)
        x = -0.000147625 + 0.999875 * jax.random.normal(jax.random.fold_in(_rk, 1), (64, 3, 224, 224), jnp.float32)
        return x
    x = _rec_inputs()

    def _L0_tok_setup():
        import jax, jax.numpy as jnp
        import numpy as np
        N_PATCHES = 14

        def _patchify(images, n_patches):
            n, c, h, w = images.shape
            ps = h // n_patches
            x = images.reshape(n, c, n_patches, ps, n_patches, ps)
            x = x.transpose(0, 2, 4, 1, 3, 5)
            return x.reshape(n, n_patches * n_patches, c * ps * ps)
        key = jax.random.key(seed)
        k1, k2, k3 = jax.random.split(key, 3)
        batch, c, h, w = (64, 3, 224, 224)
        input_dim = c * (h // N_PATCHES) * (w // N_PATCHES)
        hidden_d = 192
        images = jax.random.normal(k1, (batch, c, h, w), dtype=jnp.float32)
        W = jax.random.normal(k2, (hidden_d, input_dim), dtype=jnp.float32) * input_dim ** (-0.5)
        b = jax.random.normal(k3, (hidden_d,), dtype=jnp.float32) * 0.01
        return {'images': images, 'W': W, 'b': b}
    _L0_tok_all = _L0_tok_setup()
    _L0_tok_in = {k: v for k, v in _L0_tok_all.items() if k in ('W', 'b')}
    del _L0_tok_all

    def _L0_attn_setup():
        import jax, jax.numpy as jnp
        import numpy as np
        import math
        N_HEAD = 12
        N_EMBD = 192
        HEAD_DIM = N_EMBD // N_HEAD // 2
        DEPTH = 12
        LAMBDA_INIT = 0.8 - 0.6 * math.exp(-0.3 * DEPTH)

        def _sdpa_over_heads(q, k, v):
            scale = 1.0 / math.sqrt(q.shape[-1])
            s = jnp.einsum('bnqd,bnkd->bnqk', q, k) * scale
            a = jax.nn.softmax(s, axis=-1)
            return jnp.einsum('bnqk,bnkd->bnqd', a, v)
        key = jax.random.key(seed)
        ks = jax.random.split(key, 7)
        B, N, D = (4, 2048, N_EMBD)
        s = 0.02
        return {'x': jax.random.normal(ks[0], (B, N, D), dtype=jnp.float32), 'W_attn': jax.random.normal(ks[1], (3 * D, D), dtype=jnp.float32) * s, 'W_out': jax.random.normal(ks[2], (D, D), dtype=jnp.float32) * s, 'lambda_q1': jax.random.normal(ks[3], (HEAD_DIM,), dtype=jnp.float32) * 0.1, 'lambda_k1': jax.random.normal(ks[4], (HEAD_DIM,), dtype=jnp.float32) * 0.1, 'lambda_q2': jax.random.normal(ks[5], (HEAD_DIM,), dtype=jnp.float32) * 0.1, 'lambda_k2': jax.random.normal(ks[6], (HEAD_DIM,), dtype=jnp.float32) * 0.1}
    _L0_attn_all = _L0_attn_setup()
    _L0_attn_in = {k: v for k, v in _L0_attn_all.items() if k in ('W_attn', 'W_out', 'lambda_q1', 'lambda_k1', 'lambda_q2', 'lambda_k2')}
    del _L0_attn_all

    def _L0_ffn_setup():
        import jax, jax.numpy as jnp
        import numpy as np
        B, N, C, H, E = (8, 256, 192, 768, 4)
        key = jax.random.key(seed)
        ks = jax.random.split(key, 8)
        s_in = 1.0 / np.sqrt(C)
        s_h = 1.0 / np.sqrt(H)
        return {'x': jax.random.normal(ks[0], (B, N, C), dtype=jnp.float32), 'gate_w': jax.random.normal(ks[1], (C, E), dtype=jnp.float32) * 0.01, 'gate_b': jnp.zeros((E,), dtype=jnp.float32), 'gate_center': jnp.zeros((E,), dtype=jnp.float32), 'w1': jax.random.uniform(ks[2], (E, C, H), jnp.float32, -s_in, s_in), 'b1': jax.random.uniform(ks[3], (E, H), jnp.float32, -s_in, s_in), 'w2': jax.random.uniform(ks[4], (E, H, C), jnp.float32, -s_h, s_h), 'b2': jax.random.uniform(ks[5], (E, C), jnp.float32, -s_h, s_h)}
    _L0_ffn_all = _L0_ffn_setup()
    _L0_ffn_in = {k: v for k, v in _L0_ffn_all.items() if k in ('gate_w', 'gate_b', 'gate_center', 'w1', 'b1', 'w2', 'b2')}
    del _L0_ffn_all
    return {'x': x, 'L0_tok_W': _L0_tok_in['W'], 'L0_tok_b': _L0_tok_in['b'], 'L0_attn_W_attn': _L0_attn_in['W_attn'], 'L0_attn_W_out': _L0_attn_in['W_out'], 'L0_attn_lambda_q1': _L0_attn_in['lambda_q1'], 'L0_attn_lambda_k1': _L0_attn_in['lambda_k1'], 'L0_attn_lambda_q2': _L0_attn_in['lambda_q2'], 'L0_attn_lambda_k2': _L0_attn_in['lambda_k2'], 'L0_ffn_gate_w': _L0_ffn_in['gate_w'], 'L0_ffn_gate_b': _L0_ffn_in['gate_b'], 'L0_ffn_gate_center': _L0_ffn_in['gate_center'], 'L0_ffn_w1': _L0_ffn_in['w1'], 'L0_ffn_b1': _L0_ffn_in['b1'], 'L0_ffn_w2': _L0_ffn_in['w2'], 'L0_ffn_b2': _L0_ffn_in['b2']}

def reference(x, L0_tok_W, L0_tok_b, L0_attn_W_attn, L0_attn_W_out, L0_attn_lambda_q1, L0_attn_lambda_k1, L0_attn_lambda_q2, L0_attn_lambda_k2, L0_ffn_gate_w, L0_ffn_gate_b, L0_ffn_gate_center, L0_ffn_w1, L0_ffn_b1, L0_ffn_w2, L0_ffn_b2):
    import jax
    import jax.numpy as jnp

    def _L0_tok_ref(images, W, b):
        import jax, jax.numpy as jnp
        import numpy as np
        N_PATCHES = 14

        def _patchify(images, n_patches):
            n, c, h, w = images.shape
            ps = h // n_patches
            x = images.reshape(n, c, n_patches, ps, n_patches, ps)
            x = x.transpose(0, 2, 4, 1, 3, 5)
            return x.reshape(n, n_patches * n_patches, c * ps * ps)
        patches = _patchify(images, N_PATCHES)
        tokens = jnp.einsum('npd,hd->nph', patches, W) + b
        return tokens

    def _L0_attn_ref(x, W_attn, W_out, lambda_q1, lambda_k1, lambda_q2, lambda_k2):
        import jax, jax.numpy as jnp
        import numpy as np
        import math
        N_HEAD = 12
        N_EMBD = 192
        HEAD_DIM = N_EMBD // N_HEAD // 2
        DEPTH = 12
        LAMBDA_INIT = 0.8 - 0.6 * math.exp(-0.3 * DEPTH)

        def _sdpa_over_heads(q, k, v):
            scale = 1.0 / math.sqrt(q.shape[-1])
            s = jnp.einsum('bnqd,bnkd->bnqk', q, k) * scale
            a = jax.nn.softmax(s, axis=-1)
            return jnp.einsum('bnqk,bnkd->bnqd', a, v)
        B, N, D = x.shape
        H, hd = (N_HEAD, HEAD_DIM)
        qkv = x @ W_attn.T
        q, k, v = jnp.split(qkv, 3, axis=-1)
        q = q.reshape(B, N, H, 2, hd)
        k = k.reshape(B, N, H, 2, hd)
        v = v.reshape(B, N, H, 2 * hd)
        q1, q2 = (q[:, :, :, 0], q[:, :, :, 1])
        k1, k2 = (k[:, :, :, 0], k[:, :, :, 1])
        o1 = _sdpa_over_heads(q1, k1, v)
        o2 = _sdpa_over_heads(q2, k2, v)
        lam1 = jnp.exp(jnp.sum(lambda_q1 * lambda_k1))
        lam2 = jnp.exp(jnp.sum(lambda_q2 * lambda_k2))
        lam_full = lam1 - lam2 + LAMBDA_INIT
        y = (o1 - lam_full * o2) * (1.0 - LAMBDA_INIT)
        y = y.reshape(B, N, H * 2 * hd)
        return y @ W_out.T

    def _L0_ffn_ref(x, gate_w, gate_b, gate_center, w1, b1, w2, b2):
        import jax, jax.numpy as jnp
        import numpy as np
        B, N, C, H, E = (8, 256, 192, 768, 4)
        b, n, c = x.shape
        scores = jnp.einsum('bnc,ce->bne', x, gate_w) + gate_b
        p_experts = jax.nn.softmax(scores - gate_center, axis=-1)
        expert = jnp.argmax(p_experts, axis=-1).reshape(-1)
        xt = x.reshape(-1, c)
        h = jax.nn.gelu(jnp.einsum('tc,ech->eth', xt, w1) + b1[:, None, :], approximate=False)
        out_all = jnp.einsum('eth,ehc->etc', h, w2) + b2[:, None, :]
        out = jnp.take_along_axis(out_all, expert[None, :, None], axis=0)[0]
        return out.reshape(b, n, c)
    h = _L0_tok_ref(x, L0_tok_W, L0_tok_b)
    h = h + _L0_attn_ref(_layernorm(h, axis=-1), L0_attn_W_attn, L0_attn_W_out, L0_attn_lambda_q1, L0_attn_lambda_k1, L0_attn_lambda_q2, L0_attn_lambda_k2)
    h = h + _L0_ffn_ref(_layernorm(h, axis=-1), L0_ffn_gate_w, L0_ffn_gate_b, L0_ffn_gate_center, L0_ffn_w1, L0_ffn_b1, L0_ffn_w2, L0_ffn_b2)
    return h

_drawn_inputs = setup_inputs


def setup_inputs(seed=0):
    import zlib

    import numpy as np

    out = dict(_drawn_inputs(seed))
    spreads = {'L0_ffn_gate_b': (0.0, 0.1), 'L0_ffn_gate_center': (0.0, 0.574)}
    factors = {'L0_tok_b': 4.697,
     'L0_attn_W_attn': 8.0,
     'L0_attn_W_out': 8.0,
     'L0_attn_lambda_q1': 8.0,
     'L0_attn_lambda_k1': 8.0,
     'L0_attn_lambda_q2': 8.0,
     'L0_attn_lambda_k2': 8.0,
     'L0_ffn_b1': 20.54,
     'L0_ffn_b2': 14.753,
     'L0_ffn_gate_w': 2.681}
    for name, (base, spread) in spreads.items():
        noise = np.random.default_rng([zlib.crc32(name.encode()), seed]).standard_normal(out[name].shape)
        drawn = base * np.exp(spread * noise) if base else spread * noise
        out[name] = jnp.asarray(drawn.astype(out[name].dtype))
    for name, factor in factors.items():
        out[name] = (out[name] * factor).astype(out[name].dtype)
    return out
```

```python
import math
from contextlib import ExitStack

import concourse.bass as bass
from concourse import mybir
from concourse.alu_op_type import AluOpType as ALU

F32 = mybir.dt.float32
BF16 = mybir.dt.bfloat16
I32 = mybir.dt.int32
ACT = mybir.ActivationFunctionType
AX = mybir.AxisListType

IMAGES, CHANNELS, PIXELS, PATCH = 64, 3, 224, 16
SIDE = PIXELS // PATCH
TOK = SIDE * SIDE
N = IMAGES * TOK
IN = CHANNELS * PATCH * PATCH
D = 192
HEADS, SUBS, HD = 12, 2, 8
DV = SUBS * HD
E, HID = 4, 768
EPS = 1e-5
LAMBDA_INIT = 0.8 - 0.6 * math.exp(-0.3 * 12)
SCALE = 1.0 / math.sqrt(HD)

KD = 96
ND = D // KD
KI = IN // 128
DG = D + E

GT = 7
GTOK = GT * 128
GROUPS = N // GTOK
STEPS = 2 * GT
QKV_HALF = 3 * D // 2
PE_HEADS = 9

TILE = 512
SLOTS = TILE // 128
REGION = N + TILE
TILES = (N - E) // TILE + E
LEAST_TILES = -(-N // TILE)
SPARE = TILES - LEAST_TILES
SPARE_ROW = E * REGION
ALL_ROWS = SPARE_ROW + SPARE * TILE
ROW = D + E + 1
NO_TOKEN = 1 << 24
KH = HID // 128


def wait(engine, sem, value, passed=None):
    if isinstance(value, int):
        if value > 0:
            engine.wait_ge(sem, value)
        return
    engine.wait_ge(sem, value)
    if passed is not None:
        engine.sem_inc(passed, 1)


def prepare(nc, sem, c, a, passed):
    with ExitStack() as ctx:
        def sb(name, shape, dt=F32):
            return ctx.enter_context(nc.sbuf_tensor(name, shape, dt))

        w_nat = sb("w_nat", [KD, ND, IN])
        wo_nat = sb("wo_nat", [KD, ND, D])
        gate = sb("gate", [KD, ND, E])
        gate0 = sb("gate0", [KD, ND, E])
        bcol = sb("bcol", [KD, ND])
        brep = sb("brep", [KD, ND, 128])
        mean_w = sb("mean_w", [KD, KD])
        lam = sb("lam", [128, 4, HD])
        prod = sb("prod", [128, 2, HD])
        dots = sb("dots", [128, 2])
        edots = sb("edots", [128, 2])
        lam_d = sb("lam_d", [128, 1])
        gbias = sb("gbias", [128, 2, E])
        ones = sb("ones", [128, 128])
        p_mean = ctx.enter_context(nc.psum_tensor("p_mean", [KD, 512], F32))
        p_fold = ctx.enter_context(nc.psum_tensor("p_fold", [128, 512], F32))

        loaded, ones_set, mean_set, means, gate_less, rep_set, scaled = (
            sem(n) for n in ("p_loaded", "p_ones", "p_mean_w", "p_means", "p_gate_less", "p_rep", "p_scaled"))
        folded, lam_step, lam_exp, made, ids, wo_loaded = (
            sem(n) for n in ("p_folded", "p_lam", "p_lam_exp", "p_made", "p_ids", "p_wo_loaded"))
        LOADS = 16 * 14

        with nc.Block() as block:
            @block.sync
            def _(sp):
                sp.dma_start(w_nat[:], a["tok_W"].rearrange("(k p) i -> p k i", k=ND)).then_inc(loaded, 16)
                sp.dma_start(wo_nat[:], a["W_out"].rearrange("(k p) i -> p k i", k=ND)).then_inc(loaded, 16)
                sp.dma_start(gate[:], a["gate_w"].rearrange("(k p) e -> p k e", k=ND)).then_inc(loaded, 16)
                sp.dma_start(bcol[:], a["tok_b_col"]).then_inc(loaded, 16)
                sp.dma_start(c["WT"][:, :, 0:D], a["tok_WT"].rearrange("(k p) h -> p k h", k=KI)).then_inc(loaded, 16)
                sp.dma_start(c["bias"][:, 0:D], a["tok_b"].partition_broadcast(128)).then_inc(loaded, 16)
                sp.dma_start(c["WqkvT"][:], a["W_attnT"].rearrange("(k p) f -> p k f", k=ND)).then_inc(loaded, 16)
                sp.dma_start(c["WoT"][:, :, 0:D], a["W_outT"].rearrange("(k p) f -> p k f", k=ND)).then_inc(loaded, 16)
                for i, name in enumerate(("lambda_q1", "lambda_k1", "lambda_q2", "lambda_k2")):
                    sp.dma_start(lam[:, i, :], a[name].partition_broadcast(128)).then_inc(loaded, 16)
                sp.dma_start(gbias[:, 0, :], a["gate_b"].partition_broadcast(128)).then_inc(loaded, 16)
                sp.dma_start(gbias[:, 1, :], a["gate_center"].partition_broadcast(128)).then_inc(loaded, 16)

            @block.gpsimd
            def _(pool):
                nc.gpsimd.memset(c["ident"][:], 0.0).then_inc(ids, 1)
                nc.gpsimd.memset(ones[:], 1.0).then_inc(ids, 1)
                nc.gpsimd.memset(c["ones_b"][:], 1.0).then_inc(ids, 1)
                pool.wait_ge(ids, 3)
                nc.gpsimd.affine_select(out=c["ident"][:], in_=c["ident"][:], compare_op=ALU.not_equal, fill=1.0,
                                        base=0, pattern=[[-1, 128]], channel_multiplier=1).then_inc(ids, 1)
                nc.gpsimd.affine_select(out=c["before"][:], in_=ones[:], compare_op=ALU.is_gt, fill=0.0,
                                        base=0, pattern=[[1, 128]], channel_multiplier=-1).then_inc(ids, 1)
                nc.gpsimd.iota(c["number"][:], pattern=[[128, GT]], base=0, channel_multiplier=1,
                               allow_small_or_imprecise_dtypes=True).then_inc(ids, 1)
                pool.wait_ge(ids, 6)
                for e in range(E):
                    nc.gpsimd.memset(c["next_row"][:, e:e + 1], float(e * REGION)).then_inc(made, 1)

            @block.vector
            def _(dve):
                nc.vector.memset(mean_w[:], 1.0 / D).then_inc(mean_set, 1)
                dve.wait_ge(loaded, LOADS)
                nc.vector.tensor_copy(brep[:], bcol[:].unsqueeze(2).broadcast_to([KD, ND, 128])).then_inc(rep_set, 1)
                nc.vector.tensor_scalar(wo_nat[:], wo_nat[:], 1.0 - LAMBDA_INIT, None, ALU.mult).then_inc(scaled, 1)
                nc.vector.tensor_scalar(c["WoT"][:, :, 0:D], c["WoT"][:, :, 0:D], 1.0 - LAMBDA_INIT, None,
                                        ALU.mult).then_inc(scaled, 1)
                nc.vector.tensor_tensor(prod[:, 0, :], lam[:, 0, :], lam[:, 1, :], ALU.mult).then_inc(lam_step, 1)
                nc.vector.tensor_tensor(prod[:, 1, :], lam[:, 2, :], lam[:, 3, :], ALU.mult).then_inc(lam_step, 1)
                dve.wait_ge(lam_step, 2)
                nc.vector.reduce_sum(dots[:], prod[:], AX.X).then_inc(lam_step, 1)
                nc.vector.tensor_tensor(c["gbias"][:], gbias[:, 0, :], gbias[:, 1, :], ALU.subtract).then_inc(made, 1)
                dve.wait_ge(means, 1)
                nc.vector.tensor_tensor(gate0[:], gate[:], p_mean[:, 0:E].unsqueeze(1).broadcast_to([KD, ND, E]),
                                        ALU.subtract).then_inc(gate_less, 1)
                dve.wait_ge(lam_exp, 1)
                nc.vector.tensor_tensor(lam_d[:], edots[:, 1:2], edots[:, 0:1], ALU.subtract).then_inc(lam_step, 1)
                dve.wait_ge(lam_step, 4)
                nc.vector.tensor_scalar(c["neg_lambda"][:], lam_d[:], -LAMBDA_INIT, None, ALU.add).then_inc(made, 1)
                dve.wait_ge(folded, 1)
                nc.vector.tensor_copy(c["WT"][:, :, D:DG],
                                      p_fold[:, 0:KI * E].rearrange("p (k e) -> p k e", k=KI)).then_inc(made, 1)
                at = KI * E
                nc.vector.tensor_copy(c["WoT"][:, :, D:DG],
                                      p_fold[0:KD, at:at + ND * E].rearrange("p (k e) -> p k e", k=ND)).then_inc(made, 1)
                at += ND * E
                nc.vector.tensor_copy(c["bias"][:, D:DG], p_fold[:, at:at + E]).then_inc(made, 1)

            @block.scalar
            def _(act):
                act.wait_ge(lam_step, 3)
                nc.scalar.activation(edots[:], dots[:], ACT.Exp).then_inc(lam_exp, 1)

            @block.tensor
            def _(pe):
                pe.wait_ge(loaded, LOADS)
                pe.wait_ge(mean_set, 1)
                for k in range(ND):
                    mm = nc.tensor.matmul(p_mean[:, 0:E], mean_w[:], gate[:, k, :], start=k == 0, stop=k == ND - 1)
                mm.then_inc(means, 1)
                pe.wait_ge(gate_less, 1)
                pe.wait_ge(rep_set, 1)
                pe.wait_ge(scaled, 2)
                jobs = ([(w_nat, i * 128, 128) for i in range(KI)] + [(wo_nat, i * KD, KD) for i in range(ND)]
                        + [(brep, 0, 128)])
                for j, (w, at, m) in enumerate(jobs):
                    for k in range(ND):
                        mm = nc.tensor.matmul(p_fold[0:m, j * E:(j + 1) * E], w[:, k, at:at + m], gate0[:, k, :],
                                              start=k == 0, stop=k == ND - 1)
                mm.then_inc(folded, 1)


def attend(nc, sem, c, a, dram, passed):
    PATCH_AT, STATS_AT = 0, 0
    NORM_AT, QKV_AT = 1, 1
    SCORE_AT = 2
    PROB_AT = 3
    SUM_AT = 4
    OUT_AT = 5
    H1_AT = 6
    GATE_AT = 7
    PLACE_AT = 8
    SCATTER_AT = 14

    with ExitStack() as ctx:
        def sb(name, shape, dt=F32):
            return ctx.enter_context(nc.sbuf_tensor("at_" + name, shape, dt))

        def ps(name, shape):
            return ctx.enter_context(nc.psum_tensor("at_" + name, shape, F32))

        x_sb = [sb(f"x_sb{i}", [128, KI, GTOK]) for i in range(2)]
        h0_sb = [sb(f"h0_sb{i}", [128, DG]) for i in range(GT)]
        stats = [sb(f"stats{i}", [128, 6]) for i in range(2)]
        mv = [sb(f"mv{i}", [128, 2]) for i in range(2)]
        veps = sb("veps", [128, 1])
        rstd = [sb(f"rstd{i}", [128, 1]) for i in range(2)]
        neg_half = sb("neg_half", [128, 1])
        xn = [sb(f"xn{i}", [128, D]) for i in range(2)]
        xnT = sb("xnT", [KD, ND, 128])
        qkv = [sb(f"qkv{i}", [128, 2, 3 * D // 2]) for i in range(GT)]
        qk_prod = sb("qk_prod", [128, HEADS * HEADS * DV])
        score = [sb(f"score{i}", [128, HEADS, HEADS, SUBS]) for i in range(2)]
        top_s = [sb(f"top_s{i}", [128, HEADS, SUBS]) for i in range(2)]
        less = [sb(f"less{i}", [128, HEADS, HEADS, SUBS]) for i in range(2)]
        expo = [sb(f"expo{i}", [128, HEADS, HEADS, SUBS]) for i in range(2)]
        den = sb("den", [128, HEADS, SUBS])
        inv = sb("inv", [128, HEADS, SUBS])
        prob = sb("prob", [128, HEADS, HEADS, SUBS])
        weight = sb("weight", [128, HEADS, HEADS])
        av_prod = [sb(f"av_prod{i}", [128, HEADS, HEADS, DV]) for i in range(2)]
        y = [sb(f"y{i}", [128, D]) for i in range(2)]
        yT = sb("yT", [KD, ND, 128])
        rows = [sb(f"rows{i}", [128, GT, ROW]) for i in range(2)]
        stats_h = [sb(f"stats_h{i}", [128, 6]) for i in range(2)]
        mv_h = [sb(f"mv_h{i}", [128, GT, 2]) for i in range(2)]
        veps_h = sb("veps_h", [128, GT])
        rstd_h = sb("rstd_h", [128, GT])
        gate = sb("gate_s", [128, GT, E])
        gate_b = sb("gate_sb", [128, GT, E])
        top = sb("top", [128, GT])
        order = sb("order", [128, 1, E])
        tied = sb("tied", [128, GT, E])
        first = sb("first", [128, GT, E])
        chosen = sb("chosen", [128, GT, E])
        chosen_b = sb("chosen_b", [128, GT, E], BF16)
        place = sb("place", [128, GT, E])
        place_c = sb("place_c", [128, GT, E])
        slot = [sb(f"slot{i}", [128, GT], I32) for i in range(2)]
        number = sb("number_f", [128, GT])

        p_h = ps("p_h", [128, 512])
        p_t = ps("p_t", [KD, ND, 256])
        p_qkv = ps("p_qkv", [128, 2, 512])
        p_y = ps("p_y", [128, 512])
        p_yT = ps("p_yT", [KD, ND, 256])
        p_o = ps("p_o", [128, 512])
        p_rank = ps("p_rank", [128, 512])

        x_loaded = [sem(f"x_loaded{i}") for i in range(2)]
        scattered = [sem(f"scattered{i}") for i in range(STEPS)]
        (patch_done, h0_done, stats_done, mv_done, eps_done, rstd_done, xn_done, t_done, t_copied, qkv_done, qkv_copied,
         qk_done, score_done, top_done, less_done, exp_done, den_done, inv_done, neg_done, prob_done, weight_done,
         av_done, sum_done, y_copied, y_rest, yt_done, yt_copied, out_done, h1_done, stats_h_done, mv_h_done) = (
            sem(n) for n in (
                "patch_done", "h0_done", "stats_done", "mv_done", "eps_done", "rstd_done", "xn_done", "t_done", "t_copied",
                "qkv_done", "qkv_copied", "qk_done", "score_done", "top_done", "less_done", "exp_done", "den_done",
                "inv_done", "neg_done", "prob_done", "weight_done", "av_done", "sum_done", "y_copied", "y_rest",
                "yt_done", "yt_copied", "out_done", "h1_done", "stats_h_done", "mv_h_done"))
        (eps_h_done, rstd_h_done, gate_step, gate_done, top_e, tied_done, first_done, chosen_f, chosen_done, rank_done,
         place_done, base_done, placed, slot_done, number_set, number_next, constants) = (
            sem(n) for n in (
                "eps_h_done", "rstd_h_done", "gate_step", "gate_done", "top_e", "tied_done", "first_done", "chosen_f",
                "chosen_done", "rank_done", "place_done", "base_done", "placed", "slot_done", "number_set",
                "number_next", "constants"))

        class At:

            def __init__(self, i, u, lag):
                self.i, self.u = (i, u - lag) if u >= lag else (i - 1, u - lag + STEPS)
                self.tile = self.i * STEPS + self.u
                self.there = not isinstance(self.i, int) or (self.i >= 0 and self.tile < N // 128)
                self.two = self.u % 2
                self.slot = self.u % GT
                self.half = self.u // GT
                self.group = self.i * 2 + self.half
                self.last = self.slot == GT - 1

        def loop(engine, step):
            for i in range(2):
                for u in range(STEPS):
                    step(i, u)
            with engine.Fori(2, GROUPS // 2) as i:
                for u in range(STEPS):
                    step(i, u)
            for u in range(STEPS):
                step(GROUPS // 2, u)

        with nc.Block() as block:
            @block.sync
            def _(sp):
                def load(half, row):
                    for k in range(KI):
                        sp.dma_start(x_sb[half][:, k, :], a["xT"][k, :, bass.ds(row, GTOK)]).then_inc(x_loaded[half], 16)

                load(0, 0)
                load(1, GTOK)
                with sp.Fori(0, GROUPS // 2 - 1) as i:
                    row = [sp.snap(i * STEPS * 128 + (2 + n) * GTOK) for n in range(2)]
                    read = [sp.snap(i * STEPS + (1 + n) * GT) for n in range(2)]
                    for n in range(2):
                        wait(sp, patch_done, read[n], passed)
                        load(n, row[n])

            @block.tensor
            def _(pe):
                def step(i, u):
                    t = At(i, u, PATCH_AT)
                    if t.there:
                        if t.slot == 0:
                            pe.wait_ge(x_loaded[t.half], t.i * (16 * KI) + 16 * KI)
                        wait(pe, h0_done, t.tile)
                        for k in range(KI):
                            mm = nc.tensor.matmul(p_h[:, 0:DG], x_sb[t.half][:, k, t.slot * 128:(t.slot + 1) * 128],
                                                  c["WT"][:, k, :], start=k == 0, stop=k == KI - 1)
                        mm.then_inc(patch_done, 1)
                    t = At(i, u, OUT_AT)
                    if t.there:
                        pe.wait_ge(y_copied, t.tile + 1)
                        pe.wait_ge(y_rest, t.tile + 1)
                        wait(pe, yt_copied, t.tile)
                        for k in range(ND):
                            mm = nc.tensor.transpose(p_yT[:, k, 0:128], y[t.two][:, k * KD:(k + 1) * KD], c["ident"][:])
                        mm.then_inc(yt_done, 1)
                    t = At(i, u, NORM_AT)
                    if t.there:
                        pe.wait_ge(xn_done, t.tile + 1)
                        wait(pe, t_copied, t.tile)
                        for k in range(ND):
                            mm = nc.tensor.transpose(p_t[:, k, 0:128], xn[t.two][:, k * KD:(k + 1) * KD], c["ident"][:])
                        mm.then_inc(t_done, 1)
                    t = At(i, u, SUM_AT)
                    if t.there:
                        pe.wait_ge(av_done, t.tile + 1)
                        wait(pe, y_copied, t.tile)
                        for k in range(HEADS):
                            mm = nc.tensor.matmul(p_y[:, 0:PE_HEADS * DV], c["ident"][:], av_prod[t.two][:, 0:PE_HEADS, k, :],
                                                  start=k == 0, stop=k == HEADS - 1)
                        mm.then_inc(sum_done, 1)
                    t = At(i, u, QKV_AT)
                    if t.there:
                        pe.wait_ge(t_copied, t.tile + 1)
                        wait(pe, qkv_copied, t.tile)
                        for n in range(2):
                            for k in range(ND):
                                mm = nc.tensor.matmul(p_qkv[:, n, 0:QKV_HALF], xnT[:, k, :],
                                                      c["WqkvT"][:, k, n * QKV_HALF:(n + 1) * QKV_HALF],
                                                      start=k == 0, stop=k == ND - 1)
                        mm.then_inc(qkv_done, 1)
                    t = At(i, u, OUT_AT)
                    if t.there:
                        pe.wait_ge(yt_copied, t.tile + 1)
                        wait(pe, h1_done, t.tile)
                        for k in range(ND):
                            mm = nc.tensor.matmul(p_o[:, 0:DG], yT[:, k, :], c["WoT"][:, k, :],
                                                  start=k == 0, stop=k == ND - 1)
                        mm.then_inc(out_done, 1)
                    t = At(i, u, GATE_AT)
                    if t.there and t.last:
                        pe.wait_ge(chosen_done, t.group + 1)
                        wait(pe, base_done, t.group)
                        flat = chosen_b[:].rearrange("p j e -> p (j e)")
                        for j in range(GT):
                            nc.tensor.matmul(p_rank[:, j * E:GT * E], (c["ones_b"] if j else c["before"])[:],
                                             flat[:, 0:(GT - j) * E], start=j == 0, stop=j == GT - 1,
                                             skip_group_check=True)
                        for j in range(GT):
                            mm = nc.tensor.matmul(p_rank[:, GT * E:(GT + 1) * E], c["ones_b"][:], chosen_b[:, j, :],
                                                  start=j == 0, stop=j == GT - 1, skip_group_check=True)
                        mm.then_inc(rank_done, 1)

                loop(pe, step)

            @block.scalar
            def _(act):
                def step(i, u):
                    t = At(i, u, PROB_AT)
                    if t.there:
                        act.wait_ge(less_done, t.tile + 1)
                        nc.scalar.activation(expo[t.two][:], less[t.two][:], ACT.Exp, scale=SCALE).then_inc(exp_done, 1)
                    t = At(i, u, OUT_AT)
                    if t.there:
                        act.wait_ge(yt_done, t.tile + 1)
                        wait(act, out_done, t.tile)
                        nc.scalar.copy(yT[:], p_yT[:, :, 0:128]).then_inc(yt_copied, 1)
                    t = At(i, u, NORM_AT)
                    if t.there:
                        act.wait_ge(t_done, t.tile + 1)
                        wait(act, qkv_done, t.tile)
                        nc.scalar.copy(xnT[:], p_t[:, :, 0:128]).then_inc(t_copied, 1)
                    t = At(i, u, SUM_AT)
                    if t.there:
                        act.wait_ge(sum_done, t.tile + 1)
                        nc.scalar.copy(y[t.two][:, 0:PE_HEADS * DV], p_y[:, 0:PE_HEADS * DV]).then_inc(y_copied, 1)
                    t = At(i, u, QKV_AT)
                    if t.there:
                        act.wait_ge(qkv_done, t.tile + 1)
                        wait(act, av_done, t.tile - GT + 1)
                        nc.scalar.copy(qkv[t.slot][:], p_qkv[:, :, 0:QKV_HALF]).then_inc(qkv_copied, 1)

                loop(act, step)

            @block.vector
            def _(dve):
                def step(i, u):
                    t = At(i, u, NORM_AT)
                    if t.there:
                        dve.wait_ge(rstd_done, t.tile + 1)
                        nc.vector.tensor_scalar(xn[t.two][:], h0_sb[t.slot][:, 0:D], mv[t.two][:, 0:1], rstd[t.two][:],
                                                ALU.subtract, ALU.mult).then_inc(xn_done, 1)
                    t = At(i, u, SCORE_AT)
                    if t.there:
                        flat = qkv[t.slot][:].rearrange("p n f -> p (n f)")
                        q = flat[:, 0:D].rearrange("p (h f) -> p h f", h=HEADS).unsqueeze(2)
                        k = flat[:, D:2 * D].rearrange("p (h f) -> p h f", h=HEADS).unsqueeze(1)
                        dve.wait_ge(qkv_copied, t.tile + 1)
                        wait(dve, score_done, t.tile)
                        nc.vector.tensor_tensor(qk_prod[:].rearrange("p (h k f) -> p h k f", h=HEADS, k=HEADS),
                                                q.broadcast_to([128, HEADS, HEADS, DV]),
                                                k.broadcast_to([128, HEADS, HEADS, DV]), ALU.mult).then_inc(qk_done, 1)
                    t = At(i, u, PROB_AT)
                    if t.there:
                        dve.wait_ge(exp_done, t.tile + 1)
                        nc.vector.reduce_sum(den[:], expo[t.two][:].rearrange("p h k s -> p h s k"), AX.X)\
                            .then_inc(den_done, 1)
                    t = At(i, u, STATS_AT)
                    if t.there:
                        dve.wait_ge(patch_done, t.tile + 1)
                        nc.vector.tensor_tensor(h0_sb[t.slot][:], p_h[:, 0:DG], c["bias"][:], ALU.add).then_inc(h0_done, 1)
                    t = At(i, u, PROB_AT)
                    if t.there:
                        dve.wait_ge(den_done, t.tile + 1)
                        wait(dve, prob_done, t.tile)
                        nc.vector.reciprocal(inv[:], den[:]).then_inc(inv_done, 1)
                    t = At(i, u, STATS_AT)
                    if t.there:
                        dve.wait_ge(h0_done, t.tile + 1)
                        nc.vector.bn_stats(stats[t.two][:], h0_sb[t.slot][:, 0:D]).then_inc(stats_done, 1)
                    t = At(i, u, PROB_AT)
                    if t.there:
                        dve.wait_ge(inv_done, t.tile + 1)
                        nc.vector.tensor_scalar(inv[:, :, 1], inv[:, :, 1], c["neg_lambda"][:], None,
                                                ALU.mult).then_inc(neg_done, 1)
                    t = At(i, u, STATS_AT)
                    if t.there:
                        wait(dve, stats_done, t.tile + 1, passed)
                        nc.vector.bn_aggr(mv[t.two][:], stats[t.two][:]).then_inc(mv_done, 1)
                    t = At(i, u, PROB_AT)
                    if t.there:
                        dve.wait_ge(neg_done, t.tile + 1)
                        wait(dve, weight_done, t.tile)
                        nc.vector.tensor_tensor(prob[:], expo[t.two][:],
                                                inv[:].unsqueeze(2).broadcast_to([128, HEADS, HEADS, SUBS]),
                                                ALU.mult).then_inc(prob_done, 1)
                    t = At(i, u, H1_AT)
                    if t.there:
                        dve.wait_ge(out_done, t.tile + 1)
                        wait(dve, scattered[t.u], t.i * 16)
                        nc.vector.tensor_tensor(rows[t.half][:, t.slot, 0:DG], p_o[:, 0:DG], h0_sb[t.slot][:],
                                                ALU.add).then_inc(h1_done, 1)
                    t = At(i, u, SCORE_AT)
                    if t.there:
                        dve.wait_ge(qk_done, t.tile + 1)
                        wait(dve, less_done, t.tile - 1)
                        nc.vector.reduce_sum(score[t.two][:].rearrange("p h k s -> p (h k s)"),
                                             qk_prod[:].rearrange("p (x d) -> p x d", d=HD), AX.X).then_inc(score_done, 1)
                    t = At(i, u, H1_AT)
                    if t.there:
                        dve.wait_ge(h1_done, t.tile + 1)
                        nc.vector.bn_stats(stats_h[t.two][:], rows[t.half][:, t.slot, 0:D]).then_inc(stats_h_done, 1)
                    t = At(i, u, SUM_AT)
                    if t.there:
                        dve.wait_ge(av_done, t.tile + 1)
                        wait(dve, yt_done, t.tile - 1)
                        nc.vector.reduce_sum(y[t.two][:, PE_HEADS * DV:D].rearrange("p (h d) -> p h d", d=DV),
                                             av_prod[t.two][:, PE_HEADS:HEADS, :, :].rearrange("p h k d -> p h d k"),
                                             AX.X).then_inc(y_rest, 1)
                    t = At(i, u, SCORE_AT)
                    if t.there:
                        dve.wait_ge(score_done, t.tile + 1)
                        nc.vector.reduce_max(top_s[t.two][:], score[t.two][:].rearrange("p h k s -> p h s k"), AX.X)\
                            .then_inc(top_done, 1)
                    t = At(i, u, H1_AT)
                    if t.there:
                        if t.slot == 0:
                            wait(dve, eps_h_done, t.group)
                        wait(dve, stats_h_done, t.tile + 1, passed)
                        nc.vector.bn_aggr(mv_h[t.half][:, t.slot, :], stats_h[t.two][:]).then_inc(mv_h_done, 1)
                    t = At(i, u, GATE_AT)
                    if t.there and t.last:
                        choose(t)
                    t = At(i, u, PLACE_AT)
                    if t.there and t.last:
                        put(t)

                def choose(t):
                    g = t.group
                    dve.wait_ge(gate_done, g + 1)
                    nc.vector.reduce_max(top[:], gate_b[:], AX.X).then_inc(top_e, 1)
                    dve.wait_ge(top_e, g * 2 + 1)
                    nc.vector.tensor_tensor(tied[:], gate_b[:], top[:].unsqueeze(2).broadcast_to([128, GT, E]),
                                            ALU.is_ge).then_inc(tied_done, 1)
                    dve.wait_ge(tied_done, g + 1)
                    nc.vector.tensor_tensor(first[:], tied[:], order[:].broadcast_to([128, GT, E]),
                                            ALU.mult).then_inc(first_done, 1)
                    dve.wait_ge(first_done, g + 1)
                    nc.vector.reduce_max(top[:], first[:], AX.X).then_inc(top_e, 1)
                    dve.wait_ge(top_e, g * 2 + 2)
                    for out in (chosen, chosen_b):
                        last = nc.vector.tensor_tensor(out[:], first[:], top[:].unsqueeze(2).broadcast_to([128, GT, E]),
                                                       ALU.is_equal)
                    last.then_inc(chosen_done, 1)

                def put(t):
                    g = t.group
                    dve.wait_ge(rank_done, g + 1)
                    nc.vector.tensor_tensor(place[:], p_rank[:, 0:GT * E].rearrange("p (j e) -> p j e", j=GT),
                                            c["next_row"][:].unsqueeze(1).broadcast_to([128, GT, E]),
                                            ALU.add).then_inc(place_done, 1)
                    dve.wait_ge(place_done, g + 1)
                    nc.vector.tensor_tensor(c["next_row"][:], p_rank[:, GT * E:(GT + 1) * E], c["next_row"][:],
                                            ALU.add).then_inc(base_done, 1)
                    nc.vector.tensor_tensor(place_c[:], place[:], chosen[:], ALU.mult).then_inc(placed, 1)
                    dve.wait_ge(placed, g + 1)
                    with nc.allow_low_precision(reason="sums of whole numbers below 2^24"):
                        nc.vector.tensor_reduce(slot[t.half][:], place_c[:], AX.X, ALU.add).then_inc(slot_done, 1)

                dve.wait_ge(constants, 1 + E)
                loop(dve, step)

            @block.gpsimd
            def _(pool):
                def inverse_std(var, eps_out, out, eps_sem, out_sem, count):
                    nc.gpsimd.tensor_scalar(eps_out, var, EPS, None, ALU.add).then_inc(eps_sem, 1)
                    wait(pool, eps_sem, count, passed)
                    shape = list(var.shape)
                    nc.gpsimd.tensor_tensor(out, eps_out, neg_half[:].broadcast_to(shape), ALU.pow).then_inc(out_sem, 1)

                def step(i, u):
                    t = At(i, u, PROB_AT)
                    if t.there:
                        wait(pool, top_done, t.tile + 1, passed)
                        wait(pool, exp_done, t.tile - 1, passed)
                        nc.gpsimd.tensor_tensor(less[t.two][:], score[t.two][:],
                                                top_s[t.two][:].unsqueeze(2).broadcast_to([128, HEADS, HEADS, SUBS]),
                                                ALU.subtract).then_inc(less_done, 1)
                    t = At(i, u, SCATTER_AT)
                    if t.there:
                        if t.slot == 0:
                            wait(pool, number_next, t.group + 1, passed)
                            nc.gpsimd.tensor_copy(rows[t.half][:, :, DG:ROW], number[:].unsqueeze(2)).then_inc(number_set, 1)
                            wait(pool, number_set, t.group + 1, passed)
                            nc.gpsimd.tensor_scalar(number[:], number[:], float(GTOK), None, ALU.add)\
                                .then_inc(number_next, 1)
                            wait(pool, slot_done, t.group + 1, passed)
                        nc.gpsimd.indirect_dma_start(dram["rows"][0:ALL_ROWS, :],
                                                     bass.IndirectOffsetOnAxis(ap=slot[t.half][:, t.slot:t.slot + 1], axis=0),
                                                     rows[t.half][:, t.slot, :], None).then_inc(scattered[t.u], 16)
                    t = At(i, u, GATE_AT)
                    if t.there and t.last:
                        g = t.group
                        wait(pool, mv_h_done, t.tile + 1, passed)
                        inverse_std(mv_h[t.half][:, :, 1], veps_h[:], rstd_h[:], eps_h_done, rstd_h_done, g + 1)
                        wait(pool, rstd_h_done, g + 1, passed)
                        nc.gpsimd.tensor_tensor(gate[:], rows[t.half][:, :, D:DG],
                                                rstd_h[:].unsqueeze(2).broadcast_to([128, GT, E]),
                                                ALU.mult).then_inc(gate_step, 1)
                        wait(pool, gate_step, g + 1, passed)
                        wait(pool, chosen_done, g, passed)
                        nc.gpsimd.tensor_tensor(gate_b[:], gate[:], c["gbias"][:].unsqueeze(1).broadcast_to([128, GT, E]),
                                                ALU.add).then_inc(gate_done, 1)
                    t = At(i, u, PROB_AT)
                    if t.there:
                        wait(pool, prob_done, t.tile + 1, passed)
                        wait(pool, av_done, t.tile, passed)
                        nc.gpsimd.tensor_tensor(weight[:], prob[:, :, :, 0], prob[:, :, :, 1], ALU.add)\
                            .then_inc(weight_done, 1)
                        wait(pool, weight_done, t.tile + 1, passed)
                        wait(pool, sum_done, t.tile - 1, passed)
                        wait(pool, y_rest, t.tile - 1, passed)
                        v = qkv[t.slot][:].rearrange("p n f -> p (n f)")[:, 2 * D:3 * D]
                        nc.gpsimd.tensor_tensor(av_prod[t.two][:],
                                                weight[:].unsqueeze(3).broadcast_to([128, HEADS, HEADS, DV]),
                                                v.rearrange("p (k d) -> p k d", k=HEADS).unsqueeze(1)
                                                .broadcast_to([128, HEADS, HEADS, DV]), ALU.mult).then_inc(av_done, 1)
                    t = At(i, u, STATS_AT)
                    if t.there:
                        wait(pool, mv_done, t.tile + 1, passed)
                        wait(pool, xn_done, t.tile - 1, passed)
                        inverse_std(mv[t.two][:, 1:2], veps[:], rstd[t.two][:], eps_done, rstd_done, t.tile + 1)

                nc.gpsimd.memset(neg_half[:], -0.5).then_inc(constants, 1)
                for e in range(E):
                    nc.gpsimd.memset(order[:, :, e:e + 1], float(E - e)).then_inc(constants, 1)
                nc.gpsimd.tensor_copy(number[:], c["number"][:]).then_inc(number_next, 1)
                pool.wait_ge(constants, 1 + E)
                loop(pool, step)
                for u in range(STEPS):
                    pool.wait_ge(scattered[u], 16 * (GROUPS // 2))


def experts(nc, sem, c, a, dram, out, passed):
    with ExitStack() as ctx:
        def sb(name, shape, dt=F32):
            return ctx.enter_context(nc.sbuf_tensor("experts_" + name, shape, dt))

        def ps(name, p=128):
            return ctx.enter_context(nc.psum_tensor("experts_" + name, [p, 512], F32))

        pad = sb("pad", [128, SLOTS, ROW])
        region = sb("region", [1, E])
        filled = sb("filled", [1, E])
        limit = sb("limit", [1, LEAST_TILES])
        over = sb("over", [1, E, LEAST_TILES])
        tiles_to = sb("tiles_to", [1, E])
        tiles_of = sb("tiles_of", [1, E])
        index = sb("index", [1, TILES])
        ended = sb("ended", [1, TILES, E])
        ended_t = sb("ended_t", [1, TILES, E])
        which = sb("which", [1, TILES])
        before = sb("before_t", [1, TILES])
        offset = sb("offset", [1, TILES])
        first_row = sb("first_row", [1, TILES])
        expert_i = sb("expert_i", [1, TILES], I32)
        row_i = sb("row_i", [1, TILES], I32)
        fill_i = sb("fill_i", [1, E], I32)

        x_in = [sb(f"x_in{u}", [128, SLOTS, ROW]) for u in range(2)]
        w1 = [sb(f"w1_{u}", [KD, ND, HID]) for u in range(2)]
        w2 = [sb(f"w2_{u}", [128, KH, D]) for u in range(2)]
        b1 = [sb(f"b1_{u}", [128, KH]) for u in range(2)]
        b2 = [sb(f"b2_{u}", [128, D]) for u in range(2)]
        h1b2 = [sb(f"h1b2_{u}", [128, SLOTS, D]) for u in range(2)]
        token = [sb(f"token{u}", [128, SLOTS], I32) for u in range(2)]
        stats = sb("stats_e", [128, SLOTS, 6])
        mv = sb("mv_e", [128, SLOTS, 2])
        veps = sb("veps_e", [128, SLOTS])
        rstd = sb("rstd_e", [128, SLOTS])
        neg_half = sb("neg_half_e", [128, 1])
        xn = [sb(f"xn_e{u}", [128, SLOTS, D]) for u in range(2)]
        xnT = [sb(f"xnT_e{u}", [KD, ND, TILE]) for u in range(2)]
        hT = sb("hT", [128, KH, TILE])
        y_out = [sb(f"y_out{u}", [128, SLOTS, D]) for u in range(2)]
        p_t = [ps(f"p_te{k}", KD) for k in range(ND)]
        p_h = [ps(f"p_he{i}") for i in range(4)]
        p_o = [ps(f"p_oe{i}") for i in range(2)]

        x_loaded = [sem(f"e_x_loaded{u}") for u in range(2)]
        w_loaded = [sem(f"e_w_loaded{u}") for u in range(2)]
        written = [sem(f"e_written{u}") for u in range(2)]
        names = ("pad_set", "iota_set", "table_step", "table_done", "padded", "stats_done", "mv_done", "eps_done",
                 "rstd_done", "xn_done", "t_done", "t_copied", "up_done", "gelu_done", "down_done", "y_done",
                 "h1b2_done", "token_done", "half_set")
        (pad_set, iota_set, table_step, table_done, padded, stats_done, mv_done, eps_done, rstd_done, xn_done, t_done,
         t_copied, up_done, gelu_done, down_done, y_done, h1b2_done, token_done, half_set) = (sem("e_" + n) for n in names)
        XL, WL = 16, 16 * 4

        def loop(engine, step):
            for j in range(2):
                step(j, j)
            with engine.Fori(1, TILES // 2 - 1) as i:
                for u in range(2):
                    step(i * 2 + u, u)
            for j in range(TILES - 2, TILES):
                step(j, j % 2)

        def later(j, n=1):
            return not isinstance(j, int) or j + n < TILES

        def round_of(j, u, per):
            return (j - u) * (per // 2) + per

        with nc.Block() as block:
            @block.sync
            def _(sp):
                def load(u, row, expert):
                    sp.dma_start(x_in[u][:], dram["rows"][bass.ds(row, TILE), :].rearrange("(p i) d -> p i d", p=128))\
                        .then_inc(x_loaded[u], 16)
                    for dst, src in ((w1[u][:], a["w1"][bass.ds(expert, 1)].rearrange("o (k p) f -> p (o k) f", k=ND)),
                                     (w2[u][:], a["w2"][bass.ds(expert, 1)].rearrange("o (k p) f -> p (o k) f", k=KH)),
                                     (b1[u][:], a["b1T"][bass.ds(expert, 1)].rearrange("o p k -> (o p) k")),
                                     (b2[u][:], a["b2"][bass.ds(expert, 1)].rearrange("o d -> (o d)").partition_broadcast(128))):
                        sp.dma_start(dst, src).then_inc(w_loaded[u], 16)

                def tile_of(j):
                    return (sp.value_load(row_i[0:1, bass.ds(j, 1)], min_val=0, max_val=ALL_ROWS - TILE),
                            sp.value_load(expert_i[0:1, bass.ds(j, 1)], min_val=0, max_val=E - 1))

                sp.wait_ge(table_done, 3)
                sp.wait_ge(pad_set, 1)
                for t in range(SPARE):
                    sp.dma_start(dram["rows"][SPARE_ROW + t * TILE:SPARE_ROW + (t + 1) * TILE, :]
                                 .rearrange("(p i) d -> p i d", p=128), pad[:]).then_inc(padded, 16)
                for e in range(E):
                    row = sp.value_load(fill_i[0:1, e:e + 1], min_val=0, max_val=ALL_ROWS - TILE)
                    sp.dma_start(dram["rows"][bass.ds(row, TILE), :].rearrange("(p i) d -> p i d", p=128),
                                 pad[:]).then_inc(padded, 16)
                sp.wait_ge(padded, 16 * (SPARE + E))
                for j in range(2):
                    load(j, *tile_of(j))
                with sp.Fori(0, TILES // 2 - 1) as i:
                    for u in range(2):
                        row, expert = tile_of(i * 2 + (2 + u))
                        downs = sp.snap(i * (2 * SLOTS) + (1 + u) * SLOTS)
                        tokens = sp.snap(i * 2 + (1 + u))
                        wait(sp, down_done, downs, passed)
                        wait(sp, token_done, tokens, passed)
                        load(u, row, expert)

            @block.gpsimd
            def _(pool):
                nc.gpsimd.memset(pad[:, :, 0:DG], 0.0)
                nc.gpsimd.memset(neg_half[:], -0.5)
                nc.gpsimd.memset(pad[:, :, DG:ROW], float(NO_TOKEN)).then_inc(pad_set, 1)
                nc.gpsimd.iota(limit[:], pattern=[[TILE, LEAST_TILES]], base=0, channel_multiplier=0,
                               allow_small_or_imprecise_dtypes=True).then_inc(iota_set, 1)
                nc.gpsimd.iota(index[:], pattern=[[1, TILES]], base=0, channel_multiplier=0,
                               allow_small_or_imprecise_dtypes=True).then_inc(iota_set, 1)
                nc.gpsimd.iota(region[:], pattern=[[REGION, E]], base=0, channel_multiplier=0,
                               allow_small_or_imprecise_dtypes=True).then_inc(iota_set, 1)
                pool.wait_ge(pad_set, 1)

                def normal(j, u):
                    wait(pool, mv_done, SLOTS * (j + 1), passed)
                    wait(pool, xn_done, SLOTS * j, passed)
                    nc.gpsimd.tensor_scalar(veps[:], mv[:, :, 1], EPS, None, ALU.add).then_inc(eps_done, 1)
                    wait(pool, eps_done, j + 1, passed)
                    nc.gpsimd.tensor_tensor(rstd[:], veps[:], neg_half[:].broadcast_to([128, SLOTS]),
                                            ALU.pow).then_inc(rstd_done, 1)
                    pool.wait_ge(w_loaded[u], round_of(j, u, WL))
                    if not (isinstance(j, int) and j < 2):
                        wait(pool, written[u], (j - u) * (8 * SLOTS), passed)
                    nc.gpsimd.tensor_tensor(h1b2[u][:], x_in[u][:, :, 0:D],
                                            b2[u][:].unsqueeze(1).broadcast_to([128, SLOTS, D]),
                                            ALU.add).then_inc(h1b2_done, 1)
                    nc.gpsimd.tensor_copy(token[u][:], x_in[u][:, :, DG]).then_inc(token_done, 1)

                def step(j, u):
                    if later(j):
                        normal(j + 1, 1 - u)
                    wait(pool, token_done, j + 1, passed)
                    for i in range(SLOTS):
                        wait(pool, y_done, SLOTS * j + i + 1, passed)
                        nc.gpsimd.indirect_dma_start(out, bass.IndirectOffsetOnAxis(ap=token[u][:, i:i + 1], axis=0),
                                                     y_out[u][:, i, :], None, bounds_check=N - 1,
                                                     oob_is_err=False).then_inc(written[u], 16)

                normal(0, 0)
                loop(pool, step)
                for u in range(2):
                    pool.wait_ge(written[u], 16 * SLOTS * (TILES // 2))

            @block.vector
            def _(dve):
                done = [0]

                def then(ins):
                    done[0] += 1
                    ins.then_inc(table_step, 1)
                    dve.wait_ge(table_step, done[0])

                dve.wait_ge(iota_set, 3)
                rows = c["next_row"][0:1, :]
                nc.vector.tensor_copy(fill_i[:], rows).then_inc(table_done, 1)
                then(nc.vector.tensor_tensor(filled[:], rows, region[:], ALU.subtract))
                then(nc.vector.tensor_tensor(over[:], filled[:].unsqueeze(2).broadcast_to([1, E, LEAST_TILES]),
                                             limit[:].unsqueeze(1).broadcast_to([1, E, LEAST_TILES]), ALU.is_gt))
                then(nc.vector.reduce_sum(tiles_of[:], over[:], AX.X))
                then(nc.vector.tensor_copy(tiles_to[:, 0:1], tiles_of[:, 0:1]))
                for e in range(1, E):
                    then(nc.vector.tensor_tensor(tiles_to[:, e:e + 1], tiles_to[:, e - 1:e], tiles_of[:, e:e + 1], ALU.add))
                ends = tiles_to[:].unsqueeze(1).broadcast_to([1, TILES, E])
                then(nc.vector.tensor_tensor(ended[:], index[:].unsqueeze(2).broadcast_to([1, TILES, E]), ends, ALU.is_ge))
                then(nc.vector.reduce_sum(which[:], ended[:], AX.X))
                then(nc.vector.tensor_tensor(ended_t[:], ended[:], ends, ALU.mult))
                then(nc.vector.reduce_max(before[:], ended_t[:], AX.X))
                then(nc.vector.tensor_tensor(offset[:], index[:], before[:], ALU.subtract))
                then(nc.vector.tensor_scalar(first_row[:], which[:], float(REGION), None, ALU.mult))
                nc.vector.scalar_tensor_tensor(out=row_i[:], in0=offset[:], scalar=float(TILE), in1=first_row[:],
                                               op0=ALU.mult, op1=ALU.add).then_inc(table_done, 1)
                nc.vector.tensor_scalar(expert_i[:], which[:], float(E - 1), None, ALU.min).then_inc(table_done, 1)

                def normal(j, u):
                    wait(dve, x_loaded[u], round_of(j, u, XL))
                    for i in range(SLOTS):
                        nc.vector.bn_stats(stats[:, i, :], x_in[u][:, i, 0:D]).then_inc(stats_done, 1)
                    wait(dve, eps_done, j)
                    wait(dve, stats_done, SLOTS * (j + 1), passed)
                    for i in range(SLOTS):
                        nc.vector.bn_aggr(mv[:, i, :], stats[:, i, :]).then_inc(mv_done, 1)
                    dve.wait_ge(rstd_done, j + 1)
                    for i in range(SLOTS):
                        nc.vector.tensor_scalar(xn[u][:, i, :], x_in[u][:, i, 0:D], mv[:, i, 0:1], rstd[:, i:i + 1],
                                                ALU.subtract, ALU.mult).then_inc(xn_done, 1)

                def step(j, u):
                    if later(j):
                        normal(j + 1, 1 - u)
                    dve.wait_ge(h1b2_done, j + 1)
                    if not (isinstance(j, int) and j < 2):
                        dve.wait_ge(written[u], (j - u) * (8 * SLOTS))
                    for i in range(SLOTS):
                        dve.wait_ge(down_done, SLOTS * j + i + 1)
                        nc.vector.tensor_tensor(y_out[u][:, i, :], p_o[i % 2][:, 0:D], h1b2[u][:, i, :],
                                                ALU.add).then_inc(y_done, 1)

                normal(0, 0)
                loop(dve, step)

            @block.scalar
            def _(act):
                def copy_t(j, u):
                    for k in range(ND):
                        act.wait_ge(t_done, ND * j + k + 1)
                        nc.scalar.copy(xnT[u][:, k, :], p_t[k][:]).then_inc(t_copied, 1)

                def step(j, u):
                    for m in range(KH):
                        act.wait_ge(up_done, KH * j + m + 1)
                        if m == 0:
                            act.wait_ge(w_loaded[u], round_of(j, u, WL))
                        nc.scalar.activation(hT[:, m, :], p_h[(KH * u + m) % 4][:], ACT.Gelu,
                                             bias=b1[u][:, m:m + 1]).then_inc(gelu_done, 1)
                    if later(j):
                        copy_t(j + 1, 1 - u)

                copy_t(0, 0)
                loop(act, step)

            @block.tensor
            def _(pe):
                def transposes(j, u):
                    pe.wait_ge(xn_done, SLOTS * (j + 1))
                    wait(pe, t_copied, ND * j)
                    for k in range(ND):
                        for i in range(SLOTS):
                            mm = nc.tensor.transpose(p_t[k][:, i * 128:(i + 1) * 128], xn[u][:, i, k * KD:(k + 1) * KD],
                                                     c["ident"][:])
                        mm.then_inc(t_done, 1)

                def step(j, u):
                    pe.wait_ge(w_loaded[u], round_of(j, u, WL))
                    pe.wait_ge(t_copied, ND * (j + 1))
                    for m in range(KH):
                        wait(pe, gelu_done, KH * j + m - 3)
                        for k in range(ND):
                            mm = nc.tensor.matmul(p_h[(KH * u + m) % 4][:], w1[u][:, k, m * 128:(m + 1) * 128],
                                                  xnT[u][:, k, :], start=k == 0, stop=k == ND - 1)
                        mm.then_inc(up_done, 1)
                    if later(j):
                        transposes(j + 1, 1 - u)
                    pe.wait_ge(gelu_done, KH * (j + 1))
                    for i in range(SLOTS):
                        wait(pe, y_done, SLOTS * j + i - 1)
                        for k in range(KH):
                            mm = nc.tensor.matmul(p_o[i % 2][:, 0:D], hT[:, k, i * 128:(i + 1) * 128], w2[u][:, k, :],
                                                  start=k == 0, stop=k == KH - 1)
                        mm.then_inc(down_done, 1)

                transposes(0, 0)
                loop(pe, step)


def build(nc, a, out):
    dram = {"rows": nc.dram_tensor("rows", [ALL_ROWS, ROW], F32, kind="Internal").ap()}
    with ExitStack() as ctx:
        def sb(name, shape, dt=F32):
            return ctx.enter_context(nc.sbuf_tensor(name, shape, dt))

        def in_phase(stack):
            return lambda name: stack.enter_context(nc.semaphore(name))

        c = {
            "ident": sb("ident", [128, 128]),
            "before": sb("before", [128, 128], BF16),
            "ones_b": sb("ones_b", [128, 128], BF16),
            "number": sb("number", [128, GT]),
            "next_row": sb("next_row", [128, E]),
            "WT": sb("WT", [128, KI, DG]),
            "bias": sb("bias", [128, DG]),
            "WqkvT": sb("WqkvT", [KD, ND, 3 * D]),
            "WoT": sb("WoT", [KD, ND, DG]),
            "neg_lambda": sb("neg_lambda", [128, 1]),
            "gbias": sb("gbias_c", [128, E]),
        }
        passed = ctx.enter_context(nc.semaphore("passed"))
        for phase in (lambda sem: prepare(nc, sem, c, a, passed), lambda sem: attend(nc, sem, c, a, dram, passed), lambda sem: experts(nc, sem, c, a, dram, out, passed)):
            with ExitStack() as stack:
                phase(in_phase(stack))


def kernel(x, L0_tok_W, L0_tok_b, L0_attn_W_attn, L0_attn_W_out, L0_attn_lambda_q1, L0_attn_lambda_k1,
           L0_attn_lambda_q2, L0_attn_lambda_k2, L0_ffn_gate_w, L0_ffn_gate_b, L0_ffn_gate_center, L0_ffn_w1,
           L0_ffn_b1, L0_ffn_w2, L0_ffn_b2):
    import numpy as np
    import concourse.bacc as bacc
    from concourse.bass_utils import run_bass_kernel_spmd as run

    nc = bacc.Bacc("TRN2", target_bir_lowering=False, num_devices=1)
    x = np.asarray(x)
    patches = x.reshape(IMAGES, CHANNELS, SIDE, PATCH, SIDE, PATCH).transpose(1, 3, 5, 0, 2, 4)
    arrays = {
        "xT": patches.reshape(KI, 128, N),
        "tok_W": np.asarray(L0_tok_W), "tok_WT": np.asarray(L0_tok_W).T,
        "tok_b": np.asarray(L0_tok_b), "tok_b_col": np.asarray(L0_tok_b).reshape(ND, KD).T,
        "W_attnT": np.asarray(L0_attn_W_attn).T,
        "W_out": np.asarray(L0_attn_W_out), "W_outT": np.asarray(L0_attn_W_out).T,
        "lambda_q1": np.asarray(L0_attn_lambda_q1), "lambda_k1": np.asarray(L0_attn_lambda_k1),
        "lambda_q2": np.asarray(L0_attn_lambda_q2), "lambda_k2": np.asarray(L0_attn_lambda_k2),
        "gate_w": np.asarray(L0_ffn_gate_w), "gate_b": np.asarray(L0_ffn_gate_b),
        "gate_center": np.asarray(L0_ffn_gate_center),
        "w1": np.asarray(L0_ffn_w1), "w2": np.asarray(L0_ffn_w2),
        "b1T": np.asarray(L0_ffn_b1).reshape(E, KH, 128).transpose(0, 2, 1), "b2": np.asarray(L0_ffn_b2),
    }
    arrays = {k: np.ascontiguousarray(v) for k, v in arrays.items()}
    a = {k: nc.dram_tensor(k, list(v.shape), mybir.dt.from_np(v.dtype), kind="ExternalInput").ap()
         for k, v in arrays.items()}
    out = nc.dram_tensor("out", [N, D], F32, kind="ExternalOutput").ap()
    build(nc, a, out)
    r = run(nc, [arrays], core_ids=[0])
    return r.results[0]["out"].reshape(IMAGES, TOK, D)
```

```python
import math
from contextlib import ExitStack

import concourse.bass as bass
from concourse import mybir
from concourse.alu_op_type import AluOpType as ALU

F32 = mybir.dt.float32
BF16 = mybir.dt.bfloat16
I32 = mybir.dt.int32
ACT = mybir.ActivationFunctionType
AX = mybir.AxisListType

IMAGES, CHANNELS, PIXELS, PATCH = 64, 3, 224, 16
SIDE = PIXELS // PATCH
TOK = SIDE * SIDE
N = IMAGES * TOK
IN = CHANNELS * PATCH * PATCH
D = 192
HEADS, SUBS, HD = 12, 2, 8
DV = SUBS * HD
E, HID = 4, 768
EPS = 1e-5
LAMBDA_INIT = 0.8 - 0.6 * math.exp(-0.3 * 12)
SCALE = 1.0 / math.sqrt(HD)

KD = 96
ND = D // KD
KI = IN // 128
DG = D + E

GT = 7
GTOK = GT * 128
GROUPS = N // GTOK
STEPS = 2 * GT
QKV_HALF = 3 * D // 2
PE_HEADS = 8

TILE = 384
SLOTS = TILE // 128
REGION = N + TILE
TILES = (N - E) // TILE + E
LEAST_TILES = -(-N // TILE)
SPARE = TILES - LEAST_TILES
SPARE_ROW = E * REGION
ALL_ROWS = SPARE_ROW + SPARE * TILE
ROW = D + E + 1
NO_TOKEN = 1 << 24
KH = HID // 128


def wait(engine, sem, value, passed=None):
    if isinstance(value, int):
        if value > 0:
            engine.wait_ge(sem, value)
        return
    engine.wait_ge(sem, value)
    if passed is not None:
        engine.sem_inc(passed, 1)


def prepare(nc, sem, c, a, passed):
    with ExitStack() as ctx:
        def sb(name, shape, dt=F32):
            return ctx.enter_context(nc.sbuf_tensor(name, shape, dt))

        w_nat = sb("w_nat", [KD, ND, IN])
        wo_nat = sb("wo_nat", [KD, ND, D])
        gate = sb("gate", [KD, ND, E])
        gate0 = sb("gate0", [KD, ND, E])
        bcol = sb("bcol", [KD, ND])
        brep = sb("brep", [KD, ND, 128])
        mean_w = sb("mean_w", [KD, KD])
        lam = sb("lam", [128, 4, HD])
        prod = sb("prod", [128, 2, HD])
        dots = sb("dots", [128, 2])
        edots = sb("edots", [128, 2])
        lam_d = sb("lam_d", [128, 1])
        gbias = sb("gbias", [128, 2, E])
        ones = sb("ones", [128, 128])
        p_mean = ctx.enter_context(nc.psum_tensor("p_mean", [KD, 512], F32))
        p_fold = ctx.enter_context(nc.psum_tensor("p_fold", [128, 512], F32))

        loaded, ones_set, mean_set, means, gate_less, rep_set, scaled = (
            sem(n) for n in ("p_loaded", "p_ones", "p_mean_w", "p_means", "p_gate_less", "p_rep", "p_scaled"))
        folded, lam_step, lam_exp, made, ids, wo_loaded = (
            sem(n) for n in ("p_folded", "p_lam", "p_lam_exp", "p_made", "p_ids", "p_wo_loaded"))
        LOADS = 16 * 14

        with nc.Block() as block:
            @block.sync
            def _(sp):
                sp.dma_start(w_nat[:], a["tok_W"].rearrange("(k p) i -> p k i", k=ND)).then_inc(loaded, 16)
                sp.dma_start(wo_nat[:], a["W_out"].rearrange("(k p) i -> p k i", k=ND)).then_inc(loaded, 16)
                sp.dma_start(gate[:], a["gate_w"].rearrange("(k p) e -> p k e", k=ND)).then_inc(loaded, 16)
                sp.dma_start(bcol[:], a["tok_b_col"]).then_inc(loaded, 16)
                sp.dma_start(c["WT"][:, :, 0:D], a["tok_WT"].rearrange("(k p) h -> p k h", k=KI)).then_inc(loaded, 16)
                sp.dma_start(c["bias"][:, 0:D], a["tok_b"].partition_broadcast(128)).then_inc(loaded, 16)
                sp.dma_start(c["WqkvT"][:], a["W_attnT"].rearrange("(k p) f -> p k f", k=ND)).then_inc(loaded, 16)
                sp.dma_start(c["WoT"][:, :, 0:D], a["W_outT"].rearrange("(k p) f -> p k f", k=ND)).then_inc(loaded, 16)
                for i, name in enumerate(("lambda_q1", "lambda_k1", "lambda_q2", "lambda_k2")):
                    sp.dma_start(lam[:, i, :], a[name].partition_broadcast(128)).then_inc(loaded, 16)
                sp.dma_start(gbias[:, 0, :], a["gate_b"].partition_broadcast(128)).then_inc(loaded, 16)
                sp.dma_start(gbias[:, 1, :], a["gate_center"].partition_broadcast(128)).then_inc(loaded, 16)

                for half in range(2):
                    load_patches(sp, c, a, half, half * GTOK)

            @block.gpsimd
            def _(pool):
                nc.gpsimd.memset(c["ident"][:], 0.0).then_inc(ids, 1)
                nc.gpsimd.memset(ones[:], 1.0).then_inc(ids, 1)
                nc.gpsimd.memset(c["ones_b"][:], 1.0).then_inc(ids, 1)
                pool.wait_ge(ids, 3)
                nc.gpsimd.affine_select(out=c["ident"][:], in_=c["ident"][:], compare_op=ALU.not_equal, fill=1.0,
                                        base=0, pattern=[[-1, 128]], channel_multiplier=1).then_inc(ids, 1)
                nc.gpsimd.affine_select(out=c["before"][:], in_=ones[:], compare_op=ALU.is_gt, fill=0.0,
                                        base=0, pattern=[[1, 128]], channel_multiplier=-1).then_inc(ids, 1)
                nc.gpsimd.iota(c["number"][:], pattern=[[128, GT]], base=0, channel_multiplier=1,
                               allow_small_or_imprecise_dtypes=True).then_inc(ids, 1)
                pool.wait_ge(ids, 6)
                for e in range(E):
                    nc.gpsimd.memset(c["next_row"][:, e:e + 1], float(e * REGION)).then_inc(made, 1)

            @block.vector
            def _(dve):
                nc.vector.memset(mean_w[:], 1.0 / D).then_inc(mean_set, 1)
                dve.wait_ge(loaded, LOADS)
                nc.vector.tensor_copy(brep[:], bcol[:].unsqueeze(2).broadcast_to([KD, ND, 128])).then_inc(rep_set, 1)
                nc.vector.tensor_scalar(wo_nat[:], wo_nat[:], 1.0 - LAMBDA_INIT, None, ALU.mult).then_inc(scaled, 1)
                nc.vector.tensor_scalar(c["WoT"][:, :, 0:D], c["WoT"][:, :, 0:D], 1.0 - LAMBDA_INIT, None,
                                        ALU.mult).then_inc(scaled, 1)
                nc.vector.tensor_tensor(prod[:, 0, :], lam[:, 0, :], lam[:, 1, :], ALU.mult).then_inc(lam_step, 1)
                nc.vector.tensor_tensor(prod[:, 1, :], lam[:, 2, :], lam[:, 3, :], ALU.mult).then_inc(lam_step, 1)
                dve.wait_ge(lam_step, 2)
                nc.vector.reduce_sum(dots[:], prod[:], AX.X).then_inc(lam_step, 1)
                nc.vector.tensor_tensor(c["gbias"][:], gbias[:, 0, :], gbias[:, 1, :], ALU.subtract).then_inc(made, 1)
                dve.wait_ge(means, 1)
                nc.vector.tensor_tensor(gate0[:], gate[:], p_mean[:, 0:E].unsqueeze(1).broadcast_to([KD, ND, E]),
                                        ALU.subtract).then_inc(gate_less, 1)
                dve.wait_ge(lam_exp, 1)
                nc.vector.tensor_tensor(lam_d[:], edots[:, 1:2], edots[:, 0:1], ALU.subtract).then_inc(lam_step, 1)
                dve.wait_ge(lam_step, 4)
                nc.vector.tensor_scalar(c["neg_lambda"][:], lam_d[:], -LAMBDA_INIT, None, ALU.add).then_inc(made, 1)
                dve.wait_ge(folded, 1)
                nc.vector.tensor_copy(c["WT"][:, :, D:DG],
                                      p_fold[:, 0:KI * E].rearrange("p (k e) -> p k e", k=KI)).then_inc(made, 1)
                at = KI * E
                nc.vector.tensor_copy(c["WoT"][:, :, D:DG],
                                      p_fold[0:KD, at:at + ND * E].rearrange("p (k e) -> p k e", k=ND)).then_inc(made, 1)
                at += ND * E
                nc.vector.tensor_copy(c["bias"][:, D:DG], p_fold[:, at:at + E]).then_inc(made, 1)

            @block.scalar
            def _(act):
                act.wait_ge(lam_step, 3)
                nc.scalar.activation(edots[:], dots[:], ACT.Exp).then_inc(lam_exp, 1)

            @block.tensor
            def _(pe):
                pe.wait_ge(loaded, LOADS)
                pe.wait_ge(mean_set, 1)
                for k in range(ND):
                    mm = nc.tensor.matmul(p_mean[:, 0:E], mean_w[:], gate[:, k, :], start=k == 0, stop=k == ND - 1)
                mm.then_inc(means, 1)
                pe.wait_ge(gate_less, 1)
                pe.wait_ge(rep_set, 1)
                pe.wait_ge(scaled, 2)
                jobs = ([(w_nat, i * 128, 128) for i in range(KI)] + [(wo_nat, i * KD, KD) for i in range(ND)]
                        + [(brep, 0, 128)])
                for j, (w, at, m) in enumerate(jobs):
                    for k in range(ND):
                        mm = nc.tensor.matmul(p_fold[0:m, j * E:(j + 1) * E], w[:, k, at:at + m], gate0[:, k, :],
                                              start=k == 0, stop=k == ND - 1)
                mm.then_inc(folded, 1)


def load_patches(sp, c, a, half, row):
    for k in range(KI):
        sp.dma_start(c["x_sb"][half][:, k, :], a["xT"][k, :, bass.ds(row, GTOK)]).then_inc(c["x_loaded"][half], 16)


def attend(nc, sem, c, a, dram, passed):
    PATCH_AT, STATS_AT = 0, 0
    NORM_AT, QKV_AT = 1, 1
    SCORE_AT = 2
    PROB_AT = 3
    AV_AT = 4
    SUM_AT = 5
    OUT_AT = 6
    H1_AT = 7
    GATE_AT = 8
    SCATTER_AT = 15

    with ExitStack() as ctx:
        def sb(name, shape, dt=F32):
            return ctx.enter_context(nc.sbuf_tensor("at_" + name, shape, dt))

        def ps(name, shape):
            return ctx.enter_context(nc.psum_tensor("at_" + name, shape, F32))

        x_sb, x_loaded = c["x_sb"], c["x_loaded"]
        h0_sb = [sb(f"h0_sb{i}", [128, DG]) for i in range(GT)]
        neg_mean = [sb(f"neg_mean{i}", [128, 1]) for i in range(2)]
        squares = [sb(f"squares{i}", [128, 1]) for i in range(2)]
        shift = [sb(f"shift{i}", [128, 1]) for i in range(2)]
        unread = [sb(f"unread{i}", [128, D]) for i in range(4)]
        veps = sb("veps", [128, 1])
        rstd = [sb(f"rstd{i}", [128, 1]) for i in range(2)]
        neg_half = sb("neg_half", [128, 1])
        xn = [sb(f"xn{i}", [128, D]) for i in range(2)]
        xnT = sb("xnT", [KD, ND, 128])
        qkv = [sb(f"qkv{i}", [128, 2, 3 * D // 2]) for i in range(GT)]
        qk_prod = sb("qk_prod", [128, HEADS * HEADS * DV])
        score = [sb(f"score{i}", [128, HEADS, HEADS, SUBS]) for i in range(2)]
        top_s = [sb(f"top_s{i}", [128, HEADS, SUBS]) for i in range(2)]
        less = [sb(f"less{i}", [128, HEADS, HEADS, SUBS]) for i in range(2)]
        expo = [sb(f"expo{i}", [128, HEADS, HEADS, SUBS]) for i in range(2)]
        den = sb("den", [128, HEADS, SUBS])
        inv = sb("inv", [128, HEADS, SUBS])
        prob = [sb(f"prob{i}", [128, HEADS, HEADS, SUBS]) for i in range(2)]
        weight = sb("weight", [128, HEADS, HEADS])
        av_prod = [sb(f"av_prod{i}", [128, HEADS, HEADS, DV]) for i in range(2)]
        y = [sb(f"y{i}", [128, D]) for i in range(2)]
        yT = sb("yT", [KD, ND, 128])
        rows = [sb(f"rows{i}", [128, GT, ROW]) for i in range(2)]
        neg_mean_h = sb("neg_mean_h", [128, 1])
        squares_h = [sb(f"squares_h{i}", [128, GT]) for i in range(2)]
        veps_h = sb("veps_h", [128, GT])
        rstd_h = sb("rstd_h", [128, GT])
        gate = sb("gate_s", [128, GT, E])
        gate_b = sb("gate_sb", [128, GT, E])
        top = sb("top", [128, GT])
        order = sb("order", [128, 1, E])
        tied = sb("tied", [128, GT, E])
        first = sb("first", [128, GT, E])
        chosen = sb("chosen", [128, GT, E])
        chosen_b = sb("chosen_b", [128, GT, E], BF16)
        place = sb("place", [128, GT, E])
        place_c = sb("place_c", [128, GT, E])
        slot = [sb(f"slot{i}", [128, GT], I32) for i in range(2)]
        number = sb("number_f", [128, GT])

        pad = sb("pad", [128, SLOTS, ROW])
        region = sb("region", [1, E])
        filled = sb("filled", [1, E])
        limit = sb("limit", [1, LEAST_TILES])
        over = sb("over", [1, E, LEAST_TILES])
        tiles_to = sb("tiles_to", [1, E])
        tiles_of = sb("tiles_of", [1, E])
        index = sb("index", [1, TILES])
        ended = sb("ended", [1, TILES, E])
        ended_t = sb("ended_t", [1, TILES, E])
        which = sb("which", [1, TILES])
        before = sb("before_t", [1, TILES])
        offset = sb("offset", [1, TILES])
        first_row = sb("first_row", [1, TILES])
        expert_i, row_i, fill_i = c["expert_i"], c["row_i"], c["fill_i"]

        p_h = ps("p_h", [128, 512])
        p_t = ps("p_t", [KD, ND, 256])
        p_qkv = ps("p_qkv", [128, 2, 512])
        p_y = ps("p_y", [128, 512])
        p_yT = ps("p_yT", [KD, ND, 256])
        p_o = ps("p_o", [128, 512])
        p_rank = ps("p_rank", [128, 512])

        scattered = [sem(f"scattered{i}") for i in range(STEPS)]
        (patch_done, h0_done, mean_done, squares_done, eps_done, rstd_done, shift_done, xn_done, t_done, t_copied, qkv_done, qkv_copied,
         qk_done, score_done, top_done, less_done, exp_done, den_done, inv_done, neg_done, prob_done, weight_done,
         av_done, sum_done, y_copied, y_rest, yt_done, yt_copied, out_done, h1_done, mean_h_done, squares_h_done) = (
            sem(n) for n in (
                "patch_done", "h0_done", "mean_done", "squares_done", "eps_done", "rstd_done", "shift_done", "xn_done", "t_done", "t_copied",
                "qkv_done", "qkv_copied", "qk_done", "score_done", "top_done", "less_done", "exp_done", "den_done",
                "inv_done", "neg_done", "prob_done", "weight_done", "av_done", "sum_done", "y_copied", "y_rest",
                "yt_done", "yt_copied", "out_done", "h1_done", "mean_h_done", "squares_h_done"))
        pad_set, iota_set, table_step, table_done, padded = (
            sem(n) for n in ("pad_set", "iota_set", "table_step", "table_done", "padded"))
        (eps_h_done, rstd_h_done, gate_step, gate_done, top_e, tied_done, first_done, chosen_f, chosen_done, rank_done,
         place_done, base_done, placed, slot_done, number_set, number_next, constants) = (
            sem(n) for n in (
                "eps_h_done", "rstd_h_done", "gate_step", "gate_done", "top_e", "tied_done", "first_done", "chosen_f",
                "chosen_done", "rank_done", "place_done", "base_done", "placed", "slot_done", "number_set",
                "number_next", "constants"))

        class At:

            def __init__(self, i, u, lag):
                self.i, self.u = i + (u - lag) // STEPS, (u - lag) % STEPS
                self.tile = self.i * STEPS + self.u
                self.there = not isinstance(self.i, int) or (self.i >= 0 and self.tile < N // 128)
                self.two = self.u % 2
                self.slot = self.u % GT
                self.half = self.u // GT
                self.group = self.i * 2 + self.half
                self.last = self.slot == GT - 1

        def loop(engine, step):
            for i in range(2):
                for u in range(STEPS):
                    step(i, u)
            with engine.Fori(2, GROUPS // 2) as i:
                for u in range(STEPS):
                    step(i, u)
            for t in range(SCATTER_AT):
                step(GROUPS // 2 + t // STEPS, t % STEPS)

        with nc.Block() as block:
            @block.sync
            def _(sp):
                with sp.Fori(0, GROUPS // 2 - 1) as i:
                    row = [sp.snap(i * STEPS * 128 + (2 + n) * GTOK) for n in range(2)]
                    read = [sp.snap(i * STEPS + (1 + n) * GT) for n in range(2)]
                    for n in range(2):
                        wait(sp, patch_done, read[n], passed)
                        load_patches(sp, c, a, n, row[n])

                sp.wait_ge(table_done, 3)
                sp.wait_ge(pad_set, 2)
                for t in range(SPARE):
                    sp.dma_start(dram["rows"][SPARE_ROW + t * TILE:SPARE_ROW + (t + 1) * TILE, :]
                                 .rearrange("(p i) d -> p i d", p=128), pad[:]).then_inc(padded, 16)
                for e in range(E):
                    row = sp.value_load(fill_i[0:1, e:e + 1], min_val=0, max_val=ALL_ROWS - TILE)
                    sp.dma_start(dram["rows"][bass.ds(row, TILE), :].rearrange("(p i) d -> p i d", p=128),
                                 pad[:]).then_inc(padded, 16)
                for j in range(2):
                    load_weights(sp, c, a, j, expert_of(sp, c, j))
                sp.wait_ge(padded, 16 * (SPARE + E))

            @block.tensor
            def _(pe):
                def step(i, u):
                    t = At(i, u, PATCH_AT)
                    if t.there:
                        if t.slot == 0:
                            pe.wait_ge(x_loaded[t.half], t.i * (16 * KI) + 16 * KI)
                        wait(pe, h0_done, t.tile)
                        for k in range(KI):
                            mm = nc.tensor.matmul(p_h[:, 0:DG], x_sb[t.half][:, k, t.slot * 128:(t.slot + 1) * 128],
                                                  c["WT"][:, k, :], start=k == 0, stop=k == KI - 1)
                        mm.then_inc(patch_done, 1)
                    t = At(i, u, OUT_AT)
                    if t.there:
                        pe.wait_ge(y_copied, t.tile + 1)
                        pe.wait_ge(y_rest, t.tile + 1)
                        wait(pe, yt_copied, t.tile)
                        for k in range(ND):
                            mm = nc.tensor.transpose(p_yT[:, k, 0:128], y[t.two][:, k * KD:(k + 1) * KD], c["ident"][:])
                        mm.then_inc(yt_done, 1)
                    t = At(i, u, NORM_AT)
                    if t.there:
                        pe.wait_ge(xn_done, t.tile + 1)
                        wait(pe, t_copied, t.tile)
                        for k in range(ND):
                            mm = nc.tensor.transpose(p_t[:, k, 0:128], xn[t.two][:, k * KD:(k + 1) * KD], c["ident"][:])
                        mm.then_inc(t_done, 1)
                    t = At(i, u, SUM_AT)
                    if t.there:
                        pe.wait_ge(av_done, t.tile + 1)
                        wait(pe, y_copied, t.tile)
                        for k in range(HEADS):
                            mm = nc.tensor.matmul(p_y[:, 0:PE_HEADS * DV], c["ident"][:], av_prod[t.two][:, 0:PE_HEADS, k, :],
                                                  start=k == 0, stop=k == HEADS - 1)
                        mm.then_inc(sum_done, 1)
                    t = At(i, u, QKV_AT)
                    if t.there:
                        pe.wait_ge(t_copied, t.tile + 1)
                        wait(pe, qkv_copied, t.tile)
                        for n in range(2):
                            for k in range(ND):
                                mm = nc.tensor.matmul(p_qkv[:, n, 0:QKV_HALF], xnT[:, k, :],
                                                      c["WqkvT"][:, k, n * QKV_HALF:(n + 1) * QKV_HALF],
                                                      start=k == 0, stop=k == ND - 1)
                        mm.then_inc(qkv_done, 1)
                    t = At(i, u, OUT_AT)
                    if t.there:
                        pe.wait_ge(yt_copied, t.tile + 1)
                        wait(pe, h1_done, t.tile)
                        for k in range(ND):
                            mm = nc.tensor.matmul(p_o[:, 0:DG], yT[:, k, :], c["WoT"][:, k, :],
                                                  start=k == 0, stop=k == ND - 1)
                        mm.then_inc(out_done, 1)
                    t = At(i, u, GATE_AT)
                    if t.there and t.last:
                        pe.wait_ge(chosen_done, t.group + 1)
                        wait(pe, base_done, t.group)
                        flat = chosen_b[:].rearrange("p j e -> p (j e)")
                        for j in range(GT):
                            nc.tensor.matmul(p_rank[:, j * E:GT * E], (c["ones_b"] if j else c["before"])[:],
                                             flat[:, 0:(GT - j) * E], start=j == 0, stop=j == GT - 1,
                                             skip_group_check=True)
                        for j in range(GT):
                            mm = nc.tensor.matmul(p_rank[:, GT * E:(GT + 1) * E], c["ones_b"][:], chosen_b[:, j, :],
                                                  start=j == 0, stop=j == GT - 1, skip_group_check=True)
                        mm.then_inc(rank_done, 1)

                loop(pe, step)

            @block.scalar
            def _(act):
                def step(i, u):
                    t = At(i, u, PROB_AT)
                    if t.there:
                        act.wait_ge(less_done, t.tile + 1)
                        nc.scalar.activation(expo[t.two][:], less[t.two][:], ACT.Exp, scale=SCALE).then_inc(exp_done, 1)
                    t = At(i, u, NORM_AT)
                    if t.there:
                        act.wait_ge(shift_done, t.tile + 1)
                        wait(act, t_done, t.tile - 1)
                        nc.scalar.activation(xn[t.two][:], h0_sb[t.slot][:, 0:D], ACT.Identity, bias=shift[t.two][:],
                                             scale=rstd[t.two][:]).then_inc(xn_done, 1)
                    t = At(i, u, OUT_AT)
                    if t.there:
                        act.wait_ge(yt_done, t.tile + 1)
                        wait(act, out_done, t.tile)
                        nc.scalar.copy(yT[:], p_yT[:, :, 0:128]).then_inc(yt_copied, 1)
                    t = At(i, u, NORM_AT)
                    if t.there:
                        act.wait_ge(t_done, t.tile + 1)
                        wait(act, qkv_done, t.tile)
                        nc.scalar.copy(xnT[:], p_t[:, :, 0:128]).then_inc(t_copied, 1)
                    t = At(i, u, H1_AT)
                    if t.there:
                        row = rows[t.half][:, t.slot, 0:D]
                        act.wait_ge(h1_done, t.tile + 1)
                        wait(act, squares_h_done, t.tile)
                        nc.scalar.activation(unread[0][:], row, ACT.Copy, scale=-1.0 / D, accum_out=neg_mean_h[:])\
                            .then_inc(mean_h_done, 1)
                    t = At(i, u, PATCH_AT)
                    if t.there:
                        act.wait_ge(h0_done, t.tile + 1)
                        nc.scalar.activation(unread[1][:], h0_sb[t.slot][:, 0:D], ACT.Copy, scale=-1.0 / D,
                                             accum_out=neg_mean[t.two][:]).then_inc(mean_done, 1)
                    t = At(i, u, H1_AT)
                    if t.there:
                        if t.slot == 0:
                            wait(act, eps_h_done, t.group - 1)
                        act.wait_ge(mean_h_done, t.tile + 1)
                        nc.scalar.activation(unread[2][:], row, ACT.Square, bias=neg_mean_h[:],
                                             accum_out=squares_h[t.half][:, t.slot:t.slot + 1]).then_inc(squares_h_done, 1)
                    t = At(i, u, PATCH_AT)
                    if t.there:
                        act.wait_ge(mean_done, t.tile + 1)
                        nc.scalar.activation(unread[3][:], h0_sb[t.slot][:, 0:D], ACT.Square, bias=neg_mean[t.two][:],
                                             accum_out=squares[t.two][:]).then_inc(squares_done, 1)
                    t = At(i, u, SUM_AT)
                    if t.there:
                        act.wait_ge(sum_done, t.tile + 1)
                        wait(act, yt_done, t.tile - 1)
                        nc.scalar.copy(y[t.two][:, 0:PE_HEADS * DV], p_y[:, 0:PE_HEADS * DV]).then_inc(y_copied, 1)
                    t = At(i, u, QKV_AT)
                    if t.there:
                        act.wait_ge(qkv_done, t.tile + 1)
                        wait(act, av_done, t.tile - GT + 1)
                        nc.scalar.copy(qkv[t.slot][:], p_qkv[:, :, 0:QKV_HALF]).then_inc(qkv_copied, 1)

                loop(act, step)

            @block.vector
            def _(dve):
                def step(i, u):
                    t = At(i, u, SCORE_AT)
                    if t.there:
                        flat = qkv[t.slot][:].rearrange("p n f -> p (n f)")
                        q = flat[:, 0:D].rearrange("p (h f) -> p h f", h=HEADS).unsqueeze(2)
                        k = flat[:, D:2 * D].rearrange("p (h f) -> p h f", h=HEADS).unsqueeze(1)
                        dve.wait_ge(qkv_copied, t.tile + 1)
                        wait(dve, score_done, t.tile)
                        nc.vector.tensor_tensor(qk_prod[:].rearrange("p (h k f) -> p h k f", h=HEADS, k=HEADS),
                                                q.broadcast_to([128, HEADS, HEADS, DV]),
                                                k.broadcast_to([128, HEADS, HEADS, DV]), ALU.mult).then_inc(qk_done, 1)
                    t = At(i, u, PROB_AT)
                    if t.there:
                        dve.wait_ge(exp_done, t.tile + 1)
                        nc.vector.reduce_sum(den[:], expo[t.two][:].rearrange("p h k s -> p h s k"), AX.X)\
                            .then_inc(den_done, 1)
                    t = At(i, u, H1_AT)
                    if t.there:
                        dve.wait_ge(out_done, t.tile + 1)
                        wait(dve, scattered[t.u], t.i * 16)
                        nc.vector.tensor_tensor(rows[t.half][:, t.slot, 0:DG], p_o[:, 0:DG], h0_sb[t.slot][:],
                                                ALU.add).then_inc(h1_done, 1)
                    t = At(i, u, PROB_AT)
                    if t.there:
                        dve.wait_ge(den_done, t.tile + 1)
                        wait(dve, prob_done, t.tile)
                        nc.vector.reciprocal(inv[:], den[:]).then_inc(inv_done, 1)
                    t = At(i, u, PATCH_AT)
                    if t.there:
                        dve.wait_ge(patch_done, t.tile + 1)
                        wait(dve, h1_done, t.tile - GT + 1)
                        wait(dve, xn_done, t.tile - GT + 1)
                        nc.vector.tensor_tensor(h0_sb[t.slot][:], p_h[:, 0:DG], c["bias"][:], ALU.add).then_inc(h0_done, 1)
                    t = At(i, u, PROB_AT)
                    if t.there:
                        dve.wait_ge(inv_done, t.tile + 1)
                        nc.vector.tensor_scalar(inv[:, :, 1], inv[:, :, 1], c["neg_lambda"][:], None,
                                                ALU.mult).then_inc(neg_done, 1)
                    t = At(i, u, SUM_AT)
                    if t.there:
                        dve.wait_ge(av_done, t.tile + 1)
                        wait(dve, yt_done, t.tile - 1)
                        nc.vector.reduce_sum(y[t.two][:, PE_HEADS * DV:D].rearrange("p (h d) -> p h d", d=DV),
                                             av_prod[t.two][:, PE_HEADS:HEADS, :, :].rearrange("p h k d -> p h d k"),
                                             AX.X).then_inc(y_rest, 1)
                    t = At(i, u, PROB_AT)
                    if t.there:
                        dve.wait_ge(neg_done, t.tile + 1)
                        wait(dve, weight_done, t.tile - 1)
                        nc.vector.tensor_tensor(prob[t.two][:], expo[t.two][:],
                                                inv[:].unsqueeze(2).broadcast_to([128, HEADS, HEADS, SUBS]),
                                                ALU.mult).then_inc(prob_done, 1)
                    t = At(i, u, SCORE_AT)
                    if t.there:
                        dve.wait_ge(qk_done, t.tile + 1)
                        wait(dve, less_done, t.tile - 1)
                        nc.vector.reduce_sum(score[t.two][:].rearrange("p h k s -> p (h k s)"),
                                             qk_prod[:].rearrange("p (x d) -> p x d", d=HD), AX.X).then_inc(score_done, 1)
                    t = At(i, u, GATE_AT)
                    if t.there and t.last:
                        choose(t)
                    t = At(i, u, SCORE_AT)
                    if t.there:
                        dve.wait_ge(score_done, t.tile + 1)
                        nc.vector.reduce_max(top_s[t.two][:], score[t.two][:].rearrange("p h k s -> p h s k"), AX.X)\
                            .then_inc(top_done, 1)
                    t = At(i, u, GATE_AT)
                    if t.there and t.last:
                        put(t)

                def choose(t):
                    g = t.group
                    dve.wait_ge(gate_done, g + 1)
                    nc.vector.reduce_max(top[:], gate_b[:], AX.X).then_inc(top_e, 1)
                    dve.wait_ge(top_e, g * 2 + 1)
                    nc.vector.tensor_tensor(tied[:], gate_b[:], top[:].unsqueeze(2).broadcast_to([128, GT, E]),
                                            ALU.is_ge).then_inc(tied_done, 1)
                    dve.wait_ge(tied_done, g + 1)
                    nc.vector.tensor_tensor(first[:], tied[:], order[:].broadcast_to([128, GT, E]),
                                            ALU.mult).then_inc(first_done, 1)
                    dve.wait_ge(first_done, g + 1)
                    nc.vector.reduce_max(top[:], first[:], AX.X).then_inc(top_e, 1)
                    dve.wait_ge(top_e, g * 2 + 2)
                    for out in (chosen, chosen_b):
                        last = nc.vector.tensor_tensor(out[:], first[:], top[:].unsqueeze(2).broadcast_to([128, GT, E]),
                                                       ALU.is_equal)
                    last.then_inc(chosen_done, 1)

                def put(t):
                    g = t.group
                    dve.wait_ge(rank_done, g + 1)
                    nc.vector.tensor_tensor(place[:], p_rank[:, 0:GT * E].rearrange("p (j e) -> p j e", j=GT),
                                            c["next_row"][:].unsqueeze(1).broadcast_to([128, GT, E]),
                                            ALU.add).then_inc(place_done, 1)
                    dve.wait_ge(place_done, g + 1)
                    nc.vector.tensor_tensor(c["next_row"][:], p_rank[:, GT * E:(GT + 1) * E], c["next_row"][:],
                                            ALU.add).then_inc(base_done, 1)
                    nc.vector.tensor_tensor(place_c[:], place[:], chosen[:], ALU.mult).then_inc(placed, 1)
                    dve.wait_ge(placed, g + 1)
                    with nc.allow_low_precision(reason="sums of whole numbers below 2^24"):
                        nc.vector.tensor_reduce(slot[t.half][:], place_c[:], AX.X, ALU.add).then_inc(slot_done, 1)

                dve.wait_ge(constants, 1 + E)
                loop(dve, step)

                done = [0]

                def then(ins):
                    done[0] += 1
                    ins.then_inc(table_step, 1)
                    dve.wait_ge(table_step, done[0])

                dve.wait_ge(iota_set, 3)
                dve.wait_ge(base_done, GROUPS)
                next_row = c["next_row"][0:1, :]
                nc.vector.tensor_copy(fill_i[:], next_row).then_inc(table_done, 1)
                then(nc.vector.tensor_tensor(filled[:], next_row, region[:], ALU.subtract))
                then(nc.vector.tensor_tensor(over[:], filled[:].unsqueeze(2).broadcast_to([1, E, LEAST_TILES]),
                                             limit[:].unsqueeze(1).broadcast_to([1, E, LEAST_TILES]), ALU.is_gt))
                then(nc.vector.reduce_sum(tiles_of[:], over[:], AX.X))
                then(nc.vector.tensor_copy(tiles_to[:, 0:1], tiles_of[:, 0:1]))
                for e in range(1, E):
                    then(nc.vector.tensor_tensor(tiles_to[:, e:e + 1], tiles_to[:, e - 1:e], tiles_of[:, e:e + 1], ALU.add))
                ends = tiles_to[:].unsqueeze(1).broadcast_to([1, TILES, E])
                then(nc.vector.tensor_tensor(ended[:], index[:].unsqueeze(2).broadcast_to([1, TILES, E]), ends, ALU.is_ge))
                then(nc.vector.reduce_sum(which[:], ended[:], AX.X))
                then(nc.vector.tensor_tensor(ended_t[:], ended[:], ends, ALU.mult))
                then(nc.vector.reduce_max(before[:], ended_t[:], AX.X))
                then(nc.vector.tensor_tensor(offset[:], index[:], before[:], ALU.subtract))
                then(nc.vector.tensor_scalar(first_row[:], which[:], float(REGION), None, ALU.mult))
                nc.vector.scalar_tensor_tensor(out=row_i[:], in0=offset[:], scalar=float(TILE), in1=first_row[:],
                                               op0=ALU.mult, op1=ALU.add).then_inc(table_done, 1)
                nc.vector.tensor_scalar(expert_i[:], which[:], float(E - 1), None, ALU.min).then_inc(table_done, 1)

            @block.gpsimd
            def _(pool):
                def inverse_std(squares, eps_out, out, eps_sem, out_sem, count):
                    nc.gpsimd.tensor_scalar(eps_out, squares, 1.0 / D, EPS, ALU.mult, ALU.add).then_inc(eps_sem, 1)
                    wait(pool, eps_sem, count, passed)
                    nc.gpsimd.tensor_tensor(out, eps_out, neg_half[:].broadcast_to(list(eps_out.shape)),
                                            ALU.pow).then_inc(out_sem, 1)

                def step(i, u):
                    t = At(i, u, PROB_AT)
                    if t.there:
                        wait(pool, top_done, t.tile + 1, passed)
                        wait(pool, exp_done, t.tile - 1, passed)
                        nc.gpsimd.tensor_tensor(less[t.two][:], score[t.two][:],
                                                top_s[t.two][:].unsqueeze(2).broadcast_to([128, HEADS, HEADS, SUBS]),
                                                ALU.subtract).then_inc(less_done, 1)
                    t = At(i, u, GATE_AT)
                    if t.there and t.last:
                        g = t.group
                        wait(pool, squares_h_done, t.tile + 1, passed)
                        inverse_std(squares_h[t.half][:], veps_h[:], rstd_h[:], eps_h_done, rstd_h_done, g + 1)
                        wait(pool, rstd_h_done, g + 1, passed)
                        nc.gpsimd.tensor_tensor(gate[:], rows[t.half][:, :, D:DG],
                                                rstd_h[:].unsqueeze(2).broadcast_to([128, GT, E]),
                                                ALU.mult).then_inc(gate_step, 1)
                        wait(pool, gate_step, g + 1, passed)
                        wait(pool, chosen_done, g, passed)
                        nc.gpsimd.tensor_tensor(gate_b[:], gate[:], c["gbias"][:].unsqueeze(1).broadcast_to([128, GT, E]),
                                                ALU.add).then_inc(gate_done, 1)
                    t = At(i, u, AV_AT)
                    if t.there:
                        wait(pool, prob_done, t.tile + 1, passed)
                        wait(pool, av_done, t.tile, passed)
                        nc.gpsimd.tensor_tensor(weight[:], prob[t.two][:, :, :, 0], prob[t.two][:, :, :, 1], ALU.add)\
                            .then_inc(weight_done, 1)
                        wait(pool, weight_done, t.tile + 1, passed)
                        wait(pool, sum_done, t.tile - 1, passed)
                        wait(pool, y_rest, t.tile - 1, passed)
                        v = qkv[t.slot][:].rearrange("p n f -> p (n f)")[:, 2 * D:3 * D]
                        nc.gpsimd.tensor_tensor(av_prod[t.two][:],
                                                weight[:].unsqueeze(3).broadcast_to([128, HEADS, HEADS, DV]),
                                                v.rearrange("p (k d) -> p k d", k=HEADS).unsqueeze(1)
                                                .broadcast_to([128, HEADS, HEADS, DV]), ALU.mult).then_inc(av_done, 1)
                    t = At(i, u, PATCH_AT)
                    if t.there:
                        wait(pool, squares_done, t.tile + 1, passed)
                        wait(pool, xn_done, t.tile - 1, passed)
                        inverse_std(squares[t.two][:], veps[:], rstd[t.two][:], eps_done, rstd_done, t.tile + 1)
                        wait(pool, rstd_done, t.tile + 1, passed)
                        nc.gpsimd.tensor_tensor(shift[t.two][:], neg_mean[t.two][:], rstd[t.two][:],
                                                ALU.mult).then_inc(shift_done, 1)
                    t = At(i, u, SCATTER_AT)
                    if t.there:
                        if t.slot == 0:
                            wait(pool, number_next, t.group + 1, passed)
                            nc.gpsimd.tensor_copy(rows[t.half][:, :, DG:ROW], number[:].unsqueeze(2)).then_inc(number_set, 1)
                            wait(pool, number_set, t.group + 1, passed)
                            nc.gpsimd.tensor_scalar(number[:], number[:], float(GTOK), None, ALU.add)\
                                .then_inc(number_next, 1)
                            wait(pool, slot_done, t.group + 1, passed)
                        nc.gpsimd.indirect_dma_start(dram["rows"][0:ALL_ROWS, :],
                                                     bass.IndirectOffsetOnAxis(ap=slot[t.half][:, t.slot:t.slot + 1], axis=0),
                                                     rows[t.half][:, t.slot, :], None).then_inc(scattered[t.u], 16)
                nc.gpsimd.memset(pad[:, :, 0:DG], 0.0).then_inc(pad_set, 1)
                nc.gpsimd.memset(pad[:, :, DG:ROW], float(NO_TOKEN)).then_inc(pad_set, 1)
                nc.gpsimd.iota(limit[:], pattern=[[TILE, LEAST_TILES]], base=0, channel_multiplier=0,
                               allow_small_or_imprecise_dtypes=True).then_inc(iota_set, 1)
                nc.gpsimd.iota(index[:], pattern=[[1, TILES]], base=0, channel_multiplier=0,
                               allow_small_or_imprecise_dtypes=True).then_inc(iota_set, 1)
                nc.gpsimd.iota(region[:], pattern=[[REGION, E]], base=0, channel_multiplier=0,
                               allow_small_or_imprecise_dtypes=True).then_inc(iota_set, 1)
                pool.wait_ge(iota_set, 3)
                nc.gpsimd.memset(neg_half[:], -0.5).then_inc(constants, 1)
                for e in range(E):
                    nc.gpsimd.memset(order[:, :, e:e + 1], float(E - e)).then_inc(constants, 1)
                nc.gpsimd.tensor_copy(number[:], c["number"][:]).then_inc(number_next, 1)
                pool.wait_ge(constants, 1 + E)
                loop(pool, step)
                for u in range(STEPS):
                    pool.wait_ge(scattered[u], 16 * (GROUPS // 2))


def first_row_of(sp, c, j):
    return sp.value_load(c["row_i"][0:1, bass.ds(j, 1)], min_val=0, max_val=ALL_ROWS - TILE)


def expert_of(sp, c, j):
    return sp.value_load(c["expert_i"][0:1, bass.ds(j, 1)], min_val=0, max_val=E - 1)


def load_weights(sp, c, a, u, expert):
    one = bass.ds(expert, 1)
    for dst, src in ((c["w1"][u][:], a["w1"][one].rearrange("o (k p) f -> p (o k) f", k=ND)),
                     (c["w2"][u][:], a["w2"][one].rearrange("o (k p) f -> p (o k) f", k=KH)),
                     (c["b1"][u][:], a["b1T"][one].rearrange("o p k -> (o p) k")),
                     (c["b2"][u][:], a["b2"][one].rearrange("o d -> (o d)").partition_broadcast(128))):
        sp.dma_start(dst, src).then_inc(c["w_loaded"][u], 16)


def experts(nc, sem, c, a, dram, out, passed):
    with ExitStack() as ctx:
        def sb(name, shape, dt=F32):
            return ctx.enter_context(nc.sbuf_tensor("experts_" + name, shape, dt))

        def ps(name, p=128):
            return ctx.enter_context(nc.psum_tensor("experts_" + name, [p, 512], F32))

        x_in = [sb(f"x_in{u}", [128, SLOTS, ROW]) for u in range(2)]
        w1, w2, b1, b2, w_loaded = c["w1"], c["w2"], c["b1"], c["b2"], c["w_loaded"]
        h1b2 = [sb(f"h1b2_{u}", [128, SLOTS, D]) for u in range(2)]
        token = [sb(f"token{u}", [128, SLOTS], I32) for u in range(2)]
        stats = sb("stats_e", [128, SLOTS, 6])
        mv = sb("mv_e", [128, SLOTS, 2])
        veps = sb("veps_e", [128, SLOTS])
        rstd = sb("rstd_e", [128, SLOTS])
        neg_half = sb("neg_half_e", [128, 1])
        xn = [sb(f"xn_e{u}", [128, SLOTS, D]) for u in range(2)]
        xnT = [sb(f"xnT_e{u}", [KD, ND, TILE]) for u in range(2)]
        hT = sb("hT", [128, KH, TILE])
        y_out = [sb(f"y_out{u}", [128, SLOTS, D]) for u in range(2)]
        p_t = [ps(f"p_te{k}", KD) for k in range(ND)]
        p_h = [ps(f"p_he{i}") for i in range(4)]
        p_o = [ps(f"p_oe{i}") for i in range(2)]

        x_loaded = [sem(f"e_x_loaded{u}") for u in range(2)]
        written = [sem(f"e_written{u}") for u in range(2)]
        names = ("stats_done", "mv_done", "eps_done",
                 "rstd_done", "xn_done", "t_done", "t_copied", "up_done", "gelu_done", "down_done", "y_done",
                 "h1b2_done", "token_done", "half_set")
        (stats_done, mv_done, eps_done, rstd_done, xn_done, t_done,
         t_copied, up_done, gelu_done, down_done, y_done, h1b2_done, token_done, half_set) = (sem("e_" + n) for n in names)
        XL, WL = 16, 16 * 4

        def loop(engine, step):
            for j in range(2):
                step(j, j)
            with engine.Fori(1, TILES // 2 - 1) as i:
                for u in range(2):
                    step(i * 2 + u, u)
            for j in range(TILES - 2, TILES):
                step(j, j % 2)

        def later(j, n=1):
            return not isinstance(j, int) or j + n < TILES

        def round_of(j, u, per):
            return (j - u) * (per // 2) + per

        with nc.Block() as block:
            @block.sync
            def _(sp):
                def load_rows(u, row):
                    sp.dma_start(x_in[u][:], dram["rows"][bass.ds(row, TILE), :].rearrange("(p i) d -> p i d", p=128))\
                        .then_inc(x_loaded[u], 16)

                for j in range(2):
                    load_rows(j, first_row_of(sp, c, j))
                with sp.Fori(0, TILES // 2 - 1) as i:
                    for u in range(2):
                        row, expert = first_row_of(sp, c, i * 2 + (2 + u)), expert_of(sp, c, i * 2 + (2 + u))
                        downs = sp.snap(i * (2 * SLOTS) + (1 + u) * SLOTS)
                        tokens = sp.snap(i * 2 + (1 + u))
                        wait(sp, down_done, downs, passed)
                        wait(sp, token_done, tokens, passed)
                        load_rows(u, row)
                        load_weights(sp, c, a, u, expert)

            @block.gpsimd
            def _(pool):
                nc.gpsimd.memset(neg_half[:], -0.5).then_inc(half_set, 1)
                pool.wait_ge(half_set, 1)

                def normal(j, u):
                    wait(pool, mv_done, SLOTS * (j + 1), passed)
                    wait(pool, xn_done, SLOTS * j, passed)
                    nc.gpsimd.tensor_scalar(veps[:], mv[:, :, 1], EPS, None, ALU.add).then_inc(eps_done, 1)
                    wait(pool, eps_done, j + 1, passed)
                    nc.gpsimd.tensor_tensor(rstd[:], veps[:], neg_half[:].broadcast_to([128, SLOTS]),
                                            ALU.pow).then_inc(rstd_done, 1)
                    pool.wait_ge(w_loaded[u], round_of(j, u, WL))
                    if not (isinstance(j, int) and j < 2):
                        wait(pool, written[u], (j - u) * (8 * SLOTS), passed)
                    nc.gpsimd.tensor_tensor(h1b2[u][:], x_in[u][:, :, 0:D],
                                            b2[u][:].unsqueeze(1).broadcast_to([128, SLOTS, D]),
                                            ALU.add).then_inc(h1b2_done, 1)
                    nc.gpsimd.tensor_copy(token[u][:], x_in[u][:, :, DG]).then_inc(token_done, 1)

                def step(j, u):
                    if later(j):
                        normal(j + 1, 1 - u)
                    wait(pool, token_done, j + 1, passed)
                    for i in range(SLOTS):
                        wait(pool, y_done, SLOTS * j + i + 1, passed)
                        nc.gpsimd.indirect_dma_start(out, bass.IndirectOffsetOnAxis(ap=token[u][:, i:i + 1], axis=0),
                                                     y_out[u][:, i, :], None, bounds_check=N - 1,
                                                     oob_is_err=False).then_inc(written[u], 16)

                normal(0, 0)
                loop(pool, step)
                for u in range(2):
                    pool.wait_ge(written[u], 16 * SLOTS * (TILES // 2))

            @block.vector
            def _(dve):
                def normal(j, u):
                    wait(dve, x_loaded[u], round_of(j, u, XL))
                    for i in range(SLOTS):
                        nc.vector.bn_stats(stats[:, i, :], x_in[u][:, i, 0:D]).then_inc(stats_done, 1)
                    wait(dve, eps_done, j)
                    wait(dve, stats_done, SLOTS * (j + 1), passed)
                    for i in range(SLOTS):
                        nc.vector.bn_aggr(mv[:, i, :], stats[:, i, :]).then_inc(mv_done, 1)
                    dve.wait_ge(rstd_done, j + 1)
                    for i in range(SLOTS):
                        nc.vector.tensor_scalar(xn[u][:, i, :], x_in[u][:, i, 0:D], mv[:, i, 0:1], rstd[:, i:i + 1],
                                                ALU.subtract, ALU.mult).then_inc(xn_done, 1)

                def step(j, u):
                    if later(j):
                        normal(j + 1, 1 - u)
                    dve.wait_ge(h1b2_done, j + 1)
                    if not (isinstance(j, int) and j < 2):
                        dve.wait_ge(written[u], (j - u) * (8 * SLOTS))
                    for i in range(SLOTS):
                        dve.wait_ge(down_done, SLOTS * j + i + 1)
                        nc.vector.tensor_tensor(y_out[u][:, i, :], p_o[(SLOTS * u + i) % 2][:, 0:D], h1b2[u][:, i, :],
                                                ALU.add).then_inc(y_done, 1)

                normal(0, 0)
                loop(dve, step)

            @block.scalar
            def _(act):
                def copy_t(j, u):
                    for k in range(ND):
                        act.wait_ge(t_done, ND * j + k + 1)
                        nc.scalar.copy(xnT[u][:, k, :], p_t[k][:, 0:TILE]).then_inc(t_copied, 1)

                def step(j, u):
                    for m in range(KH):
                        act.wait_ge(up_done, KH * j + m + 1)
                        if m == 0:
                            act.wait_ge(w_loaded[u], round_of(j, u, WL))
                        nc.scalar.activation(hT[:, m, :], p_h[(KH * u + m) % 4][:, 0:TILE], ACT.Gelu,
                                             bias=b1[u][:, m:m + 1]).then_inc(gelu_done, 1)
                    if later(j):
                        copy_t(j + 1, 1 - u)

                copy_t(0, 0)
                loop(act, step)

            @block.tensor
            def _(pe):
                def transposes(j, u):
                    pe.wait_ge(xn_done, SLOTS * (j + 1))
                    wait(pe, t_copied, ND * j)
                    for k in range(ND):
                        for i in range(SLOTS):
                            mm = nc.tensor.transpose(p_t[k][:, i * 128:(i + 1) * 128], xn[u][:, i, k * KD:(k + 1) * KD],
                                                     c["ident"][:])
                        mm.then_inc(t_done, 1)

                def step(j, u):
                    pe.wait_ge(w_loaded[u], round_of(j, u, WL))
                    pe.wait_ge(t_copied, ND * (j + 1))
                    for m in range(KH):
                        wait(pe, gelu_done, KH * j + m - 3)
                        for k in range(ND):
                            mm = nc.tensor.matmul(p_h[(KH * u + m) % 4][:, 0:TILE], w1[u][:, k, m * 128:(m + 1) * 128],
                                                  xnT[u][:, k, :], start=k == 0, stop=k == ND - 1)
                        mm.then_inc(up_done, 1)
                    if later(j):
                        transposes(j + 1, 1 - u)
                    pe.wait_ge(gelu_done, KH * (j + 1))
                    for i in range(SLOTS):
                        wait(pe, y_done, SLOTS * j + i - 1)
                        for k in range(KH):
                            mm = nc.tensor.matmul(p_o[(SLOTS * u + i) % 2][:, 0:D], hT[:, k, i * 128:(i + 1) * 128], w2[u][:, k, :],
                                                  start=k == 0, stop=k == KH - 1)
                        mm.then_inc(down_done, 1)

                transposes(0, 0)
                loop(pe, step)


def build(nc, a, out):
    dram = {"rows": nc.dram_tensor("rows", [ALL_ROWS, ROW], F32, kind="Internal").ap()}
    with ExitStack() as ctx:
        def sb(name, shape, dt=F32):
            return ctx.enter_context(nc.sbuf_tensor(name, shape, dt))

        def in_phase(stack):
            return lambda name: stack.enter_context(nc.semaphore(name))

        c = {
            "ident": sb("ident", [128, 128]),
            "before": sb("before", [128, 128], BF16),
            "ones_b": sb("ones_b", [128, 128], BF16),
            "number": sb("number", [128, GT]),
            "next_row": sb("next_row", [128, E]),
            "WT": sb("WT", [128, KI, DG]),
            "bias": sb("bias", [128, DG]),
            "WqkvT": sb("WqkvT", [KD, ND, 3 * D]),
            "WoT": sb("WoT", [KD, ND, DG]),
            "neg_lambda": sb("neg_lambda", [128, 1]),
            "gbias": sb("gbias_c", [128, E]),
            "x_sb": [sb(f"x_sb{i}", [128, KI, GTOK]) for i in range(2)],
            "x_loaded": [ctx.enter_context(nc.semaphore(f"x_loaded{i}")) for i in range(2)],
            "expert_i": sb("expert_i", [1, TILES], I32),
            "row_i": sb("row_i", [1, TILES], I32),
            "fill_i": sb("fill_i", [1, E], I32),
            "w1": [sb(f"w1_{u}", [KD, ND, HID]) for u in range(2)],
            "w2": [sb(f"w2_{u}", [128, KH, D]) for u in range(2)],
            "b1": [sb(f"b1_{u}", [128, KH]) for u in range(2)],
            "b2": [sb(f"b2_{u}", [128, D]) for u in range(2)],
            "w_loaded": [ctx.enter_context(nc.semaphore(f"w_loaded{u}")) for u in range(2)],
        }
        passed = ctx.enter_context(nc.semaphore("passed"))
        for phase in (lambda sem: prepare(nc, sem, c, a, passed), lambda sem: attend(nc, sem, c, a, dram, passed), lambda sem: experts(nc, sem, c, a, dram, out, passed)):
            with ExitStack() as stack:
                phase(in_phase(stack))


def kernel(x, L0_tok_W, L0_tok_b, L0_attn_W_attn, L0_attn_W_out, L0_attn_lambda_q1, L0_attn_lambda_k1,
           L0_attn_lambda_q2, L0_attn_lambda_k2, L0_ffn_gate_w, L0_ffn_gate_b, L0_ffn_gate_center, L0_ffn_w1,
           L0_ffn_b1, L0_ffn_w2, L0_ffn_b2):
    import numpy as np
    import concourse.bacc as bacc
    from concourse.bass_utils import run_bass_kernel_spmd as run

    nc = bacc.Bacc("TRN2", target_bir_lowering=False, num_devices=1)
    x = np.asarray(x)
    patches = x.reshape(IMAGES, CHANNELS, SIDE, PATCH, SIDE, PATCH).transpose(1, 3, 5, 0, 2, 4)
    arrays = {
        "xT": patches.reshape(KI, 128, N),
        "tok_W": np.asarray(L0_tok_W), "tok_WT": np.asarray(L0_tok_W).T,
        "tok_b": np.asarray(L0_tok_b), "tok_b_col": np.asarray(L0_tok_b).reshape(ND, KD).T,
        "W_attnT": np.asarray(L0_attn_W_attn).T,
        "W_out": np.asarray(L0_attn_W_out), "W_outT": np.asarray(L0_attn_W_out).T,
        "lambda_q1": np.asarray(L0_attn_lambda_q1), "lambda_k1": np.asarray(L0_attn_lambda_k1),
        "lambda_q2": np.asarray(L0_attn_lambda_q2), "lambda_k2": np.asarray(L0_attn_lambda_k2),
        "gate_w": np.asarray(L0_ffn_gate_w), "gate_b": np.asarray(L0_ffn_gate_b),
        "gate_center": np.asarray(L0_ffn_gate_center),
        "w1": np.asarray(L0_ffn_w1), "w2": np.asarray(L0_ffn_w2),
        "b1T": np.asarray(L0_ffn_b1).reshape(E, KH, 128).transpose(0, 2, 1), "b2": np.asarray(L0_ffn_b2),
    }
    arrays = {k: np.ascontiguousarray(v) for k, v in arrays.items()}
    a = {k: nc.dram_tensor(k, list(v.shape), mybir.dt.from_np(v.dtype), kind="ExternalInput").ap()
         for k, v in arrays.items()}
    out = nc.dram_tensor("out", [N, D], F32, kind="ExternalOutput").ap()
    build(nc, a, out)
    r = run(nc, [arrays], core_ids=[0])
    return r.results[0]["out"].reshape(IMAGES, TOK, D)
```

```python
import math
from contextlib import ExitStack

import concourse.bass as bass
from concourse import mybir
from concourse.alu_op_type import AluOpType as ALU

F32 = mybir.dt.float32
BF16 = mybir.dt.bfloat16
F32R = mybir.dt.float32r
I32 = mybir.dt.int32
ACT = mybir.ActivationFunctionType
AX = mybir.AxisListType

IMAGES, CHANNELS, PIXELS, PATCH = 64, 3, 224, 16
SIDE = PIXELS // PATCH
TOK = SIDE * SIDE
N = IMAGES * TOK
IN = CHANNELS * PATCH * PATCH
D = 192
HEADS, SUBS, HD = 12, 2, 8
DV = SUBS * HD
E, HID = 4, 768
EPS = 1e-5
LAMBDA_INIT = 0.8 - 0.6 * math.exp(-0.3 * 12)
SCALE = 1.0 / math.sqrt(HD)

KD = 96
ND = D // KD
KI = IN // 128
DG = D + E

GT = 7
GTOK = GT * 128
GROUPS = N // GTOK
STEPS = 2 * GT
QKV_HALF = 3 * D // 2
PE_HEADS = 9

TILE = 384
SLOTS = TILE // 128
REGION = N + TILE
TILES = (N - E) // TILE + E
LEAST_TILES = -(-N // TILE)
SPARE = TILES - LEAST_TILES
SPARE_ROW = E * REGION
ALL_ROWS = SPARE_ROW + SPARE * TILE
ROW = D + E + 1
NO_TOKEN = 1 << 24
KH = HID // 128
UPPER = -4096
HIGH_LOW = ((0, 0), (0, 1), (1, 0))


def wait(engine, sem, value, passed=None):
    if isinstance(value, int):
        if value > 0:
            engine.wait_ge(sem, value)
        return
    engine.wait_ge(sem, value)
    if passed is not None:
        engine.sem_inc(passed, 1)


def prepare(nc, sem, c, a, passed):
    with ExitStack() as ctx:
        def sb(name, shape, dt=F32):
            return ctx.enter_context(nc.sbuf_tensor(name, shape, dt))

        w_nat = sb("w_nat", [KD, ND, IN])
        wo_nat = sb("wo_nat", [KD, ND, D])
        gate = sb("gate", [KD, ND, E])
        gate0 = sb("gate0", [KD, ND, E])
        bcol = sb("bcol", [KD, ND])
        brep = sb("brep", [KD, ND, 128])
        mean_w = sb("mean_w", [KD, KD])
        lam = sb("lam", [128, 4, HD])
        prod = sb("prod", [128, 2, HD])
        dots = sb("dots", [128, 2])
        edots = sb("edots", [128, 2])
        lam_d = sb("lam_d", [128, 1])
        gbias = sb("gbias", [128, 2, E])
        ones = sb("ones", [128, 128])
        p_mean = ctx.enter_context(nc.psum_tensor("p_mean", [KD, 512], F32))
        p_fold = ctx.enter_context(nc.psum_tensor("p_fold", [128, 512], F32))

        loaded, ones_set, mean_set, means, gate_less, rep_set, scaled = (
            sem(n) for n in ("p_loaded", "p_ones", "p_mean_w", "p_means", "p_gate_less", "p_rep", "p_scaled"))
        folded, lam_step, lam_exp, made, ids, wo_loaded = (
            sem(n) for n in ("p_folded", "p_lam", "p_lam_exp", "p_made", "p_ids", "p_wo_loaded"))
        LOADS = 16 * 14

        with nc.Block() as block:
            @block.sync
            def _(sp):
                sp.dma_start(w_nat[:], a["tok_W"].rearrange("(k p) i -> p k i", k=ND)).then_inc(loaded, 16)
                sp.dma_start(wo_nat[:], a["W_out"].rearrange("(k p) i -> p k i", k=ND)).then_inc(loaded, 16)
                sp.dma_start(gate[:], a["gate_w"].rearrange("(k p) e -> p k e", k=ND)).then_inc(loaded, 16)
                sp.dma_start(bcol[:], a["tok_b_col"]).then_inc(loaded, 16)
                sp.dma_start(c["WT"][:, :, 0:D], a["tok_WT"].rearrange("(k p) h -> p k h", k=KI)).then_inc(loaded, 16)
                sp.dma_start(c["bias"][:, 0:D], a["tok_b"].partition_broadcast(128)).then_inc(loaded, 16)
                sp.dma_start(c["WqkvT"][:], a["W_attnT"].rearrange("(k p) f -> p k f", k=ND)).then_inc(loaded, 16)
                sp.dma_start(c["WoT"][:, :, 0:D], a["W_outT"].rearrange("(k p) f -> p k f", k=ND)).then_inc(loaded, 16)
                for i, name in enumerate(("lambda_q1", "lambda_k1", "lambda_q2", "lambda_k2")):
                    sp.dma_start(lam[:, i, :], a[name].partition_broadcast(128)).then_inc(loaded, 16)
                sp.dma_start(gbias[:, 0, :], a["gate_b"].partition_broadcast(128)).then_inc(loaded, 16)
                sp.dma_start(gbias[:, 1, :], a["gate_center"].partition_broadcast(128)).then_inc(loaded, 16)

                for half in range(2):
                    load_patches(sp, c, a, half, half * GTOK)

            @block.gpsimd
            def _(pool):
                nc.gpsimd.memset(c["ident"][:], 0.0).then_inc(ids, 1)
                nc.gpsimd.memset(ones[:], 1.0).then_inc(ids, 1)
                nc.gpsimd.memset(c["ones_b"][:], 1.0).then_inc(ids, 1)
                pool.wait_ge(ids, 3)
                nc.gpsimd.affine_select(out=c["ident"][:], in_=c["ident"][:], compare_op=ALU.not_equal, fill=1.0,
                                        base=0, pattern=[[-1, 128]], channel_multiplier=1).then_inc(ids, 1)
                nc.gpsimd.affine_select(out=c["before"][:], in_=ones[:], compare_op=ALU.is_gt, fill=0.0,
                                        base=0, pattern=[[1, 128]], channel_multiplier=-1).then_inc(ids, 1)
                nc.gpsimd.iota(c["number"][:], pattern=[[128, GT]], base=0, channel_multiplier=1,
                               allow_small_or_imprecise_dtypes=True).then_inc(ids, 1)
                pool.wait_ge(ids, 6)
                for e in range(E):
                    nc.gpsimd.memset(c["next_row"][:, e:e + 1], float(e * REGION)).then_inc(made, 1)

            @block.vector
            def _(dve):
                nc.vector.memset(mean_w[:], 1.0 / D).then_inc(mean_set, 1)
                dve.wait_ge(loaded, LOADS)
                nc.vector.tensor_copy(brep[:], bcol[:].unsqueeze(2).broadcast_to([KD, ND, 128])).then_inc(rep_set, 1)
                nc.vector.tensor_scalar(wo_nat[:], wo_nat[:], 1.0 - LAMBDA_INIT, None, ALU.mult).then_inc(scaled, 1)
                nc.vector.tensor_scalar(c["WoT"][:, :, 0:D], c["WoT"][:, :, 0:D], 1.0 - LAMBDA_INIT, None,
                                        ALU.mult).then_inc(scaled, 1)
                nc.vector.tensor_tensor(prod[:, 0, :], lam[:, 0, :], lam[:, 1, :], ALU.mult).then_inc(lam_step, 1)
                nc.vector.tensor_tensor(prod[:, 1, :], lam[:, 2, :], lam[:, 3, :], ALU.mult).then_inc(lam_step, 1)
                dve.wait_ge(lam_step, 2)
                nc.vector.reduce_sum(dots[:], prod[:], AX.X).then_inc(lam_step, 1)
                nc.vector.tensor_tensor(c["gbias"][:], gbias[:, 0, :], gbias[:, 1, :], ALU.subtract).then_inc(made, 1)
                dve.wait_ge(means, 1)
                nc.vector.tensor_tensor(gate0[:], gate[:], p_mean[:, 0:E].unsqueeze(1).broadcast_to([KD, ND, E]),
                                        ALU.subtract).then_inc(gate_less, 1)
                dve.wait_ge(lam_exp, 1)
                nc.vector.tensor_tensor(lam_d[:], edots[:, 1:2], edots[:, 0:1], ALU.subtract).then_inc(lam_step, 1)
                dve.wait_ge(lam_step, 4)
                nc.vector.tensor_scalar(c["neg_lambda"][:], lam_d[:], -LAMBDA_INIT, None, ALU.add).then_inc(made, 1)
                dve.wait_ge(folded, 1)
                nc.vector.tensor_copy(c["WT"][:, :, D:DG],
                                      p_fold[:, 0:KI * E].rearrange("p (k e) -> p k e", k=KI)).then_inc(made, 1)
                at = KI * E
                nc.vector.tensor_copy(c["WoT"][:, :, D:DG],
                                      p_fold[0:KD, at:at + ND * E].rearrange("p (k e) -> p k e", k=ND)).then_inc(made, 1)
                at += ND * E
                nc.vector.tensor_copy(c["bias"][:, D:DG], p_fold[:, at:at + E]).then_inc(made, 1)

            @block.scalar
            def _(act):
                act.wait_ge(lam_step, 3)
                nc.scalar.activation(edots[:], dots[:], ACT.Exp).then_inc(lam_exp, 1)

            @block.tensor
            def _(pe):
                pe.wait_ge(loaded, LOADS)
                pe.wait_ge(mean_set, 1)
                for k in range(ND):
                    mm = nc.tensor.matmul(p_mean[:, 0:E], mean_w[:], gate[:, k, :], start=k == 0, stop=k == ND - 1)
                mm.then_inc(means, 1)
                pe.wait_ge(gate_less, 1)
                pe.wait_ge(rep_set, 1)
                pe.wait_ge(scaled, 2)
                jobs = ([(w_nat, i * 128, 128) for i in range(KI)] + [(wo_nat, i * KD, KD) for i in range(ND)]
                        + [(brep, 0, 128)])
                for j, (w, at, m) in enumerate(jobs):
                    for k in range(ND):
                        mm = nc.tensor.matmul(p_fold[0:m, j * E:(j + 1) * E], w[:, k, at:at + m], gate0[:, k, :],
                                              start=k == 0, stop=k == ND - 1)
                mm.then_inc(folded, 1)


def load_patches(sp, c, a, half, row):
    for k in range(KI):
        sp.dma_start(c["x_sb"][half][:, k, :], a["xT"][k, :, bass.ds(row, GTOK)]).then_inc(c["x_loaded"][half], 16)


def attend(nc, sem, c, a, dram, passed):
    PATCH_AT = 0
    STD_AT = 1
    NORM_AT, QKV_AT = 3, 3
    SCORE_AT = 4
    PROB_AT = 5
    AV_AT = 6
    SUM_AT = 7
    OUT_AT = 8
    H1_AT = 9
    GATE_AT = 10
    CHOICE_AT = 11
    PLACE_AT = 12
    SCATTER_AT = 19

    with ExitStack() as ctx:
        def sb(name, shape, dt=F32):
            return ctx.enter_context(nc.sbuf_tensor("at_" + name, shape, dt))

        def ps(name, shape):
            return ctx.enter_context(nc.psum_tensor("at_" + name, shape, F32))

        x_sb, x_loaded = c["x_sb"], c["x_loaded"]
        h0_sb = [sb(f"h0_sb{i}", [128, DG]) for i in range(STEPS)]
        neg_mean = sb("neg_mean", [128, STEPS])
        squares = sb("squares", [128, STEPS])
        rstd = sb("rstd", [128, STEPS])
        shift = sb("shift", [128, STEPS])
        veps = sb("veps", [128, 2])
        unread = [sb(f"unread{i}", [128, D]) for i in range(4)]
        neg_half = sb("neg_half", [128, 1])
        xn = [sb(f"xn{i}", [128, D]) for i in range(2)]
        xnT = sb("xnT", [KD, ND, 128])
        qkv = [sb(f"qkv{i}", [128, 2, 3 * D // 2]) for i in range(GT)]
        qk_prod = sb("qk_prod", [128, HEADS * HEADS * DV])
        score = [sb(f"score{i}", [128, HEADS, HEADS, SUBS]) for i in range(2)]
        top_s = [sb(f"top_s{i}", [128, HEADS, SUBS]) for i in range(2)]
        less = [sb(f"less{i}", [128, HEADS, HEADS, SUBS]) for i in range(2)]
        expo = [sb(f"expo{i}", [128, HEADS, HEADS, SUBS]) for i in range(2)]
        den = sb("den", [128, HEADS, SUBS])
        inv = sb("inv", [128, HEADS, SUBS])
        prob = [sb(f"prob{i}", [128, HEADS, HEADS, SUBS]) for i in range(2)]
        weight = sb("weight", [128, HEADS, HEADS])
        av_prod = [sb(f"av_prod{i}", [128, HEADS, HEADS, DV]) for i in range(2)]
        y = [sb(f"y{i}", [128, D]) for i in range(2)]
        yT = sb("yT", [KD, ND, 128])
        rows = [sb(f"rows{i}", [128, GT, ROW]) for i in range(2)]
        neg_mean_h = sb("neg_mean_h", [128, 1])
        squares_h = [sb(f"squares_h{i}", [128, GT]) for i in range(2)]
        veps_h = sb("veps_h", [128, GT])
        rstd_h = sb("rstd_h", [128, GT])
        gate = sb("gate_s", [128, GT, E])
        gate_b = sb("gate_sb", [128, GT, E])
        top = sb("top", [128, GT])
        order = sb("order", [128, 1, E])
        tied = sb("tied", [128, GT, E])
        first = sb("first", [128, GT, E])
        chosen = sb("chosen", [128, GT, E])
        chosen_b = sb("chosen_b", [128, GT, E], BF16)
        place = sb("place", [128, GT, E])
        place_c = sb("place_c", [128, GT, E])
        slot = [sb(f"slot{i}", [128, GT], I32) for i in range(2)]
        number = sb("number_f", [128, GT])

        pad = sb("pad", [128, SLOTS, ROW])
        region = sb("region", [1, E])
        filled = sb("filled", [1, E])
        limit = sb("limit", [1, LEAST_TILES])
        over = sb("over", [1, E, LEAST_TILES])
        tiles_to = sb("tiles_to", [1, E])
        tiles_of = sb("tiles_of", [1, E])
        index = sb("index", [1, TILES])
        ended = sb("ended", [1, TILES, E])
        ended_t = sb("ended_t", [1, TILES, E])
        which = sb("which", [1, TILES])
        before = sb("before_t", [1, TILES])
        offset = sb("offset", [1, TILES])
        first_row = sb("first_row", [1, TILES])
        expert_i, row_i, fill_i = c["expert_i"], c["row_i"], c["fill_i"]

        p_h = ps("p_h", [128, 512])
        p_t = ps("p_t", [KD, ND, 256])
        p_qkv = ps("p_qkv", [128, 2, 512])
        p_y = ps("p_y", [128, 512])
        p_yT = ps("p_yT", [KD, ND, 256])
        p_o = ps("p_o", [128, 512])
        p_rank = ps("p_rank", [128, 512])

        scattered = [sem(f"scattered{i}") for i in range(STEPS)]
        (patch_done, h0_done, mean_done, squares_done, eps_done, rstd_done, shift_done, xn_done, t_done, t_copied,
         qkv_done, qkv_copied, qk_done, score_done, top_done, less_done, exp_done, den_done, inv_done, neg_done, prob_done, weight_done,
         av_done, sum_done, y_copied, y_rest, yt_done, yt_copied, out_done, h1_done, mean_h_done, squares_h_done) = (
            sem(n) for n in (
                "patch_done", "h0_done", "mean_done", "squares_done", "eps_done", "rstd_done", "shift_done", "xn_done",
                "t_done", "t_copied",
                "qkv_done", "qkv_copied", "qk_done", "score_done", "top_done", "less_done", "exp_done", "den_done",
                "inv_done", "neg_done", "prob_done", "weight_done", "av_done", "sum_done", "y_copied", "y_rest",
                "yt_done", "yt_copied", "out_done", "h1_done", "mean_h_done", "squares_h_done"))
        pad_set, iota_set, table_step, table_done, padded = (
            sem(n) for n in ("pad_set", "iota_set", "table_step", "table_done", "padded"))
        (eps_h_done, rstd_h_done, gate_step, gate_done, top_e, tied_done, first_done, chosen_done, rank_done,
         place_done, base_done, placed, slot_done, number_set, number_next, constants) = (
            sem(n) for n in (
                "eps_h_done", "rstd_h_done", "gate_step", "gate_done", "top_e", "tied_done", "first_done",
                "chosen_done", "rank_done", "place_done", "base_done", "placed", "slot_done", "number_set",
                "number_next", "constants"))

        class At:

            def __init__(self, i, u, lag):
                self.i, self.u = i + (u - lag) // STEPS, (u - lag) % STEPS
                self.tile = self.i * STEPS + self.u
                self.there = not isinstance(self.i, int) or (self.i >= 0 and self.tile < N // 128)
                self.two = self.u % 2
                self.slot = self.u % GT
                self.half = self.u // GT
                self.group = self.i * 2 + self.half
                self.last = self.slot == GT - 1
                self.one = slice(self.u, self.u + 1)
                self.pair = self.i * (STEPS // 2) + self.u // 2

        def loop(engine, step):
            for i in range(2):
                for u in range(STEPS):
                    step(i, u)
            with engine.Fori(2, GROUPS // 2) as i:
                for u in range(STEPS):
                    step(i, u)
            for t in range(SCATTER_AT):
                step(GROUPS // 2 + t // STEPS, t % STEPS)

        with nc.Block() as block:
            @block.sync
            def _(sp):
                sp.wait_ge(pad_set, 2)
                for t in range(SPARE):
                    sp.dma_start(dram["rows"][SPARE_ROW + t * TILE:SPARE_ROW + (t + 1) * TILE, :]
                                 .rearrange("(p i) d -> p i d", p=128), pad[:]).then_inc(padded, 16)
                with sp.Fori(0, GROUPS // 2 - 1) as i:
                    row = [sp.snap(i * STEPS * 128 + (2 + n) * GTOK) for n in range(2)]
                    read = [sp.snap(i * STEPS + (1 + n) * GT) for n in range(2)]
                    for n in range(2):
                        wait(sp, patch_done, read[n], passed)
                        load_patches(sp, c, a, n, row[n])

                sp.wait_ge(table_done, 3)
                for e in range(E):
                    row = sp.value_load(fill_i[0:1, e:e + 1], min_val=0, max_val=ALL_ROWS - TILE)
                    sp.dma_start(dram["rows"][bass.ds(row, TILE), :].rearrange("(p i) d -> p i d", p=128),
                                 pad[:]).then_inc(padded, 16)
                for j in range(2):
                    expert = expert_of(sp, c, j)
                    load_w1(sp, c, a, j, expert)
                    load_w2(sp, c, a, j, expert)
                sp.wait_ge(padded, 16 * (SPARE + E))

            @block.tensor
            def _(pe):
                def step(i, u):
                    t = At(i, u, PATCH_AT)
                    if t.there:
                        if t.slot == 0:
                            pe.wait_ge(x_loaded[t.half], t.i * (16 * KI) + 16 * KI)
                        wait(pe, h0_done, t.tile)
                        for k in range(KI):
                            mm = nc.tensor.matmul(p_h[:, 0:DG], x_sb[t.half][:, k, t.slot * 128:(t.slot + 1) * 128],
                                                  c["WT"][:, k, :], start=k == 0, stop=k == KI - 1)
                        mm.then_inc(patch_done, 1)
                    t = At(i, u, OUT_AT)
                    if t.there:
                        pe.wait_ge(y_copied, t.tile + 1)
                        pe.wait_ge(y_rest, t.tile + 1)
                        wait(pe, yt_copied, t.tile)
                        for k in range(ND):
                            mm = nc.tensor.transpose(p_yT[:, k, 0:128], y[t.two][:, k * KD:(k + 1) * KD], c["ident"][:])
                        mm.then_inc(yt_done, 1)
                    t = At(i, u, NORM_AT)
                    if t.there:
                        pe.wait_ge(xn_done, t.tile + 1)
                        wait(pe, t_copied, t.tile)
                        for k in range(ND):
                            mm = nc.tensor.transpose(p_t[:, k, 0:128], xn[t.two][:, k * KD:(k + 1) * KD], c["ident"][:])
                        mm.then_inc(t_done, 1)
                    t = At(i, u, PLACE_AT)
                    if t.there and t.last:
                        pe.wait_ge(chosen_done, t.group + 1)
                        wait(pe, base_done, t.group)
                        flat = chosen_b[:].rearrange("p j e -> p (j e)")
                        for j in range(GT):
                            nc.tensor.matmul(p_rank[:, j * E:GT * E], (c["ones_b"] if j else c["before"])[:],
                                             flat[:, 0:(GT - j) * E], start=j == 0, stop=j == GT - 1,
                                             skip_group_check=True)
                        for j in range(GT):
                            mm = nc.tensor.matmul(p_rank[:, GT * E:(GT + 1) * E], c["ones_b"][:], chosen_b[:, j, :],
                                                  start=j == 0, stop=j == GT - 1, skip_group_check=True)
                        mm.then_inc(rank_done, 1)
                    t = At(i, u, SUM_AT)
                    if t.there:
                        pe.wait_ge(av_done, t.tile + 1)
                        wait(pe, y_copied, t.tile)
                        for k in range(HEADS):
                            mm = nc.tensor.matmul(p_y[:, 0:PE_HEADS * DV], c["ident"][:],
                                                  av_prod[t.two][:, 0:PE_HEADS, k, :], start=k == 0, stop=k == HEADS - 1)
                        mm.then_inc(sum_done, 1)
                    t = At(i, u, QKV_AT)
                    if t.there:
                        pe.wait_ge(t_copied, t.tile + 1)
                        wait(pe, qkv_copied, t.tile)
                        for n in range(2):
                            for k in range(ND):
                                mm = nc.tensor.matmul(p_qkv[:, n, 0:QKV_HALF], xnT[:, k, :],
                                                      c["WqkvT"][:, k, n * QKV_HALF:(n + 1) * QKV_HALF],
                                                      start=k == 0, stop=k == ND - 1)
                        mm.then_inc(qkv_done, 1)
                    t = At(i, u, OUT_AT)
                    if t.there:
                        pe.wait_ge(yt_copied, t.tile + 1)
                        wait(pe, h1_done, t.tile)
                        for k in range(ND):
                            mm = nc.tensor.matmul(p_o[:, 0:DG], yT[:, k, :], c["WoT"][:, k, :],
                                                  start=k == 0, stop=k == ND - 1)
                        mm.then_inc(out_done, 1)

                loop(pe, step)

            @block.scalar
            def _(act):
                def step(i, u):
                    t = At(i, u, NORM_AT)
                    if t.there:
                        act.wait_ge(shift_done, t.pair + 1)
                        wait(act, t_done, t.tile - 1)
                        nc.scalar.activation(xn[t.two][:], h0_sb[t.u][:, 0:D], ACT.Identity, bias=shift[:, t.one],
                                             scale=rstd[:, t.one]).then_inc(xn_done, 1)
                    t = At(i, u, OUT_AT)
                    if t.there:
                        act.wait_ge(yt_done, t.tile + 1)
                        wait(act, out_done, t.tile)
                        nc.scalar.copy(yT[:], p_yT[:, :, 0:128]).then_inc(yt_copied, 1)
                    t = At(i, u, NORM_AT)
                    if t.there:
                        act.wait_ge(t_done, t.tile + 1)
                        wait(act, qkv_done, t.tile)
                        nc.scalar.copy(xnT[:], p_t[:, :, 0:128]).then_inc(t_copied, 1)
                    t = At(i, u, PROB_AT)
                    if t.there:
                        act.wait_ge(less_done, t.tile + 1)
                        nc.scalar.activation(expo[t.two][:], less[t.two][:], ACT.Exp, scale=SCALE).then_inc(exp_done, 1)
                    t = At(i, u, PROB_AT)
                    if t.there:
                        act.wait_ge(inv_done, t.tile + 1)
                        nc.scalar.activation(inv[:, :, 1], inv[:, :, 1], ACT.Copy,
                                             scale=c["neg_lambda"][:]).then_inc(neg_done, 1)
                    t = At(i, u, H1_AT)
                    if t.there:
                        row = rows[t.half][:, t.slot, 0:D]
                        act.wait_ge(h1_done, t.tile + 1)
                        wait(act, squares_h_done, t.tile)
                        nc.scalar.activation(unread[0][:], row, ACT.Copy, scale=-1.0 / D, accum_out=neg_mean_h[:])\
                            .then_inc(mean_h_done, 1)
                    t = At(i, u, PATCH_AT)
                    if t.there:
                        act.wait_ge(h0_done, t.tile + 1)
                        nc.scalar.activation(unread[1][:], h0_sb[t.u][:, 0:D], ACT.Copy, scale=-1.0 / D,
                                             accum_out=neg_mean[:, t.one]).then_inc(mean_done, 1)
                    t = At(i, u, H1_AT)
                    if t.there:
                        if t.slot == 0:
                            wait(act, eps_h_done, t.group - 1)
                        act.wait_ge(mean_h_done, t.tile + 1)
                        nc.scalar.activation(unread[2][:], row, ACT.Square, bias=neg_mean_h[:],
                                             accum_out=squares_h[t.half][:, t.slot:t.slot + 1]).then_inc(squares_h_done, 1)
                    t = At(i, u, PATCH_AT)
                    if t.there:
                        act.wait_ge(mean_done, t.tile + 1)
                        nc.scalar.activation(unread[3][:], h0_sb[t.u][:, 0:D], ACT.Square, bias=neg_mean[:, t.one],
                                             accum_out=squares[:, t.one]).then_inc(squares_done, 1)
                    t = At(i, u, SUM_AT)
                    if t.there:
                        act.wait_ge(sum_done, t.tile + 1)
                        wait(act, yt_done, t.tile - 1)
                        nc.scalar.copy(y[t.two][:, 0:PE_HEADS * DV], p_y[:, 0:PE_HEADS * DV]).then_inc(y_copied, 1)
                    t = At(i, u, QKV_AT)
                    if t.there:
                        act.wait_ge(qkv_done, t.tile + 1)
                        wait(act, av_done, t.tile - GT + 1)
                        nc.scalar.copy(qkv[t.slot][:], p_qkv[:, :, 0:QKV_HALF]).then_inc(qkv_copied, 1)

                loop(act, step)

            @block.vector
            def _(dve):
                def step(i, u):
                    t = At(i, u, SCORE_AT)
                    if t.there:
                        dve.wait_ge(qkv_copied, t.tile + 1)
                        wait(dve, score_done, t.tile)
                        flat = qkv[t.slot][:].rearrange("p n f -> p (n f)")
                        q = flat[:, 0:D].rearrange("p (h f) -> p h f", h=HEADS).unsqueeze(2)
                        k = flat[:, D:2 * D].rearrange("p (h f) -> p h f", h=HEADS).unsqueeze(1)
                        nc.vector.tensor_tensor(qk_prod[:].rearrange("p (h k f) -> p h k f", h=HEADS, k=HEADS),
                                                q.broadcast_to([128, HEADS, HEADS, DV]),
                                                k.broadcast_to([128, HEADS, HEADS, DV]), ALU.mult).then_inc(qk_done, 1)
                    t = At(i, u, H1_AT)
                    if t.there:
                        dve.wait_ge(out_done, t.tile + 1)
                        wait(dve, scattered[t.u], t.i * 16)
                        nc.vector.tensor_tensor(rows[t.half][:, t.slot, 0:DG], p_o[:, 0:DG], h0_sb[t.u][:],
                                                ALU.add).then_inc(h1_done, 1)
                    t = At(i, u, PATCH_AT)
                    if t.there:
                        dve.wait_ge(patch_done, t.tile + 1)
                        wait(dve, h1_done, t.tile - STEPS + 1)
                        wait(dve, xn_done, t.tile - STEPS + 1)
                        nc.vector.tensor_tensor(h0_sb[t.u][:], p_h[:, 0:DG], c["bias"][:], ALU.add).then_inc(h0_done, 1)
                    t = At(i, u, PROB_AT)
                    if t.there:
                        dve.wait_ge(exp_done, t.tile + 1)
                        nc.vector.reduce_sum(den[:], expo[t.two][:].rearrange("p h k s -> p h s k"), AX.X)\
                            .then_inc(den_done, 1)
                    choose(At(i, u, CHOICE_AT), 0)
                    t = At(i, u, PROB_AT)
                    if t.there:
                        dve.wait_ge(den_done, t.tile + 1)
                        wait(dve, prob_done, t.tile)
                        nc.vector.reciprocal(inv[:], den[:]).then_inc(inv_done, 1)
                    t = At(i, u, SUM_AT)
                    if t.there:
                        dve.wait_ge(av_done, t.tile + 1)
                        wait(dve, yt_done, t.tile - 1)
                        nc.vector.reduce_sum(y[t.two][:, PE_HEADS * DV:D].rearrange("p (h d) -> p h d", d=DV),
                                             av_prod[t.two][:, PE_HEADS:HEADS, :, :].rearrange("p h k d -> p h d k"),
                                             AX.X).then_inc(y_rest, 1)
                    choose(At(i, u, CHOICE_AT), 1)
                    put(At(i, u, PLACE_AT), 0)
                    t = At(i, u, PROB_AT)
                    if t.there:
                        dve.wait_ge(neg_done, t.tile + 1)
                        wait(dve, weight_done, t.tile - 1)
                        nc.vector.tensor_tensor(prob[t.two][:], expo[t.two][:],
                                                inv[:].unsqueeze(2).broadcast_to([128, HEADS, HEADS, SUBS]),
                                                ALU.mult).then_inc(prob_done, 1)
                    choose(At(i, u, CHOICE_AT), 2)
                    put(At(i, u, PLACE_AT), 1)
                    t = At(i, u, SCORE_AT)
                    if t.there:
                        dve.wait_ge(qk_done, t.tile + 1)
                        wait(dve, less_done, t.tile - 1)
                        nc.vector.reduce_sum(score[t.two][:].rearrange("p h k s -> p (h k s)"),
                                             qk_prod[:].rearrange("p (x d) -> p x d", d=HD), AX.X).then_inc(score_done, 1)
                    choose(At(i, u, CHOICE_AT), 3)
                    t = At(i, u, SCORE_AT)
                    if t.there:
                        dve.wait_ge(score_done, t.tile + 1)
                        nc.vector.reduce_max(top_s[t.two][:], score[t.two][:].rearrange("p h k s -> p h s k"), AX.X)\
                            .then_inc(top_done, 1)
                    choose(At(i, u, CHOICE_AT), 4)
                    put(At(i, u, PLACE_AT), 2)

                def choose(t, part):
                    if not (t.there and t.last):
                        return
                    g = t.group
                    if part == 0:
                        dve.wait_ge(gate_done, g + 1)
                        nc.vector.reduce_max(top[:], gate_b[:], AX.X).then_inc(top_e, 1)
                    if part == 1:
                        dve.wait_ge(top_e, g * 2 + 1)
                        nc.vector.tensor_tensor(tied[:], gate_b[:], top[:].unsqueeze(2).broadcast_to([128, GT, E]),
                                                ALU.is_ge).then_inc(tied_done, 1)
                    if part == 2:
                        dve.wait_ge(tied_done, g + 1)
                        nc.vector.tensor_tensor(first[:], tied[:], order[:].broadcast_to([128, GT, E]),
                                                ALU.mult).then_inc(first_done, 1)
                    if part == 3:
                        dve.wait_ge(first_done, g + 1)
                        nc.vector.reduce_max(top[:], first[:], AX.X).then_inc(top_e, 1)
                    if part == 4:
                        dve.wait_ge(top_e, g * 2 + 2)
                        for out in (chosen, chosen_b):
                            last = nc.vector.tensor_tensor(out[:], first[:], top[:].unsqueeze(2).broadcast_to([128, GT, E]),
                                                           ALU.is_equal)
                        last.then_inc(chosen_done, 1)

                def put(t, part):
                    if not (t.there and t.last):
                        return
                    g = t.group
                    if part == 0:
                        dve.wait_ge(rank_done, g + 1)
                        nc.vector.tensor_tensor(place[:], p_rank[:, 0:GT * E].rearrange("p (j e) -> p j e", j=GT),
                                                c["next_row"][:].unsqueeze(1).broadcast_to([128, GT, E]),
                                                ALU.add).then_inc(place_done, 1)
                    if part == 1:
                        dve.wait_ge(place_done, g + 1)
                        nc.vector.tensor_tensor(c["next_row"][:], p_rank[:, GT * E:(GT + 1) * E], c["next_row"][:],
                                                ALU.add).then_inc(base_done, 1)
                        nc.vector.tensor_tensor(place_c[:], place[:], chosen[:], ALU.mult).then_inc(placed, 1)
                    if part == 2:
                        dve.wait_ge(placed, g + 1)
                        with nc.allow_low_precision(reason="sums of whole numbers below 2^24"):
                            nc.vector.tensor_reduce(slot[t.half][:], place_c[:], AX.X, ALU.add).then_inc(slot_done, 1)

                dve.wait_ge(constants, 1 + E)
                loop(dve, step)

                done = [0]

                def then(ins):
                    done[0] += 1
                    ins.then_inc(table_step, 1)
                    dve.wait_ge(table_step, done[0])

                dve.wait_ge(iota_set, 3)
                dve.wait_ge(base_done, GROUPS)
                next_row = c["next_row"][0:1, :]
                nc.vector.tensor_copy(fill_i[:], next_row).then_inc(table_done, 1)
                then(nc.vector.tensor_tensor(filled[:], next_row, region[:], ALU.subtract))
                then(nc.vector.tensor_tensor(over[:], filled[:].unsqueeze(2).broadcast_to([1, E, LEAST_TILES]),
                                             limit[:].unsqueeze(1).broadcast_to([1, E, LEAST_TILES]), ALU.is_gt))
                then(nc.vector.reduce_sum(tiles_of[:], over[:], AX.X))
                then(nc.vector.tensor_copy(tiles_to[:, 0:1], tiles_of[:, 0:1]))
                for e in range(1, E):
                    then(nc.vector.tensor_tensor(tiles_to[:, e:e + 1], tiles_to[:, e - 1:e], tiles_of[:, e:e + 1], ALU.add))
                ends = tiles_to[:].unsqueeze(1).broadcast_to([1, TILES, E])
                then(nc.vector.tensor_tensor(ended[:], index[:].unsqueeze(2).broadcast_to([1, TILES, E]), ends, ALU.is_ge))
                then(nc.vector.reduce_sum(which[:], ended[:], AX.X))
                then(nc.vector.tensor_tensor(ended_t[:], ended[:], ends, ALU.mult))
                then(nc.vector.reduce_max(before[:], ended_t[:], AX.X))
                then(nc.vector.tensor_tensor(offset[:], index[:], before[:], ALU.subtract))
                then(nc.vector.tensor_scalar(first_row[:], which[:], float(REGION), None, ALU.mult))
                nc.vector.scalar_tensor_tensor(out=row_i[:], in0=offset[:], scalar=float(TILE), in1=first_row[:],
                                               op0=ALU.mult, op1=ALU.add).then_inc(table_done, 1)
                nc.vector.tensor_scalar(expert_i[:], which[:], float(E - 1), None, ALU.min).then_inc(table_done, 1)

            @block.gpsimd
            def _(pool):
                def inverse_std(squares, eps_out, out, eps_sem, out_sem, count):
                    nc.gpsimd.tensor_scalar(eps_out, squares, 1.0 / D, EPS, ALU.mult, ALU.add).then_inc(eps_sem, 1)
                    wait(pool, eps_sem, count, passed)
                    nc.gpsimd.tensor_tensor(out, eps_out, neg_half[:].broadcast_to(list(eps_out.shape)),
                                            ALU.pow).then_inc(out_sem, 1)

                def step(i, u):
                    t = At(i, u, PROB_AT)
                    if t.there:
                        wait(pool, top_done, t.tile + 1, passed)
                        wait(pool, exp_done, t.tile - 1, passed)
                        nc.gpsimd.tensor_tensor(less[t.two][:], score[t.two][:],
                                                top_s[t.two][:].unsqueeze(2).broadcast_to([128, HEADS, HEADS, SUBS]),
                                                ALU.subtract).then_inc(less_done, 1)
                    t = At(i, u, STD_AT)
                    if t.there and t.two:
                        both = slice(t.u - 1, t.u + 1)
                        wait(pool, squares_done, t.tile + 1, passed)
                        inverse_std(squares[:, both], veps[:], rstd[:, both], eps_done, rstd_done, t.pair + 1)
                        wait(pool, rstd_done, t.pair + 1, passed)
                        nc.gpsimd.tensor_tensor(shift[:, both], neg_mean[:, both], rstd[:, both],
                                                ALU.mult).then_inc(shift_done, 1)
                    t = At(i, u, AV_AT)
                    if t.there:
                        wait(pool, prob_done, t.tile + 1, passed)
                        wait(pool, av_done, t.tile, passed)
                        nc.gpsimd.tensor_tensor(weight[:], prob[t.two][:, :, :, 0], prob[t.two][:, :, :, 1], ALU.add)\
                            .then_inc(weight_done, 1)
                        wait(pool, weight_done, t.tile + 1, passed)
                        wait(pool, sum_done, t.tile - 1, passed)
                        wait(pool, y_rest, t.tile - 1, passed)
                        v = qkv[t.slot][:].rearrange("p n f -> p (n f)")[:, 2 * D:3 * D]
                        nc.gpsimd.tensor_tensor(av_prod[t.two][:],
                                                weight[:].unsqueeze(3).broadcast_to([128, HEADS, HEADS, DV]),
                                                v.rearrange("p (k d) -> p k d", k=HEADS).unsqueeze(1)
                                                .broadcast_to([128, HEADS, HEADS, DV]), ALU.mult).then_inc(av_done, 1)
                    t = At(i, u, SCATTER_AT)
                    if t.there:
                        if t.slot == 0:
                            wait(pool, number_next, t.group + 1, passed)
                            nc.gpsimd.tensor_copy(rows[t.half][:, :, DG:ROW], number[:].unsqueeze(2)).then_inc(number_set, 1)
                            wait(pool, number_set, t.group + 1, passed)
                            nc.gpsimd.tensor_scalar(number[:], number[:], float(GTOK), None, ALU.add)\
                                .then_inc(number_next, 1)
                            wait(pool, slot_done, t.group + 1, passed)
                        to = slot[t.half][:, t.slot:t.slot + 1]
                        nc.gpsimd.indirect_dma_start(dram["rows"][0:ALL_ROWS, :], bass.IndirectOffsetOnAxis(ap=to, axis=0),
                                                     rows[t.half][:, t.slot, :], None).then_inc(scattered[t.u], 16)
                    t = At(i, u, GATE_AT)
                    if t.there and t.last:
                        g = t.group
                        wait(pool, squares_h_done, t.tile + 1, passed)
                        inverse_std(squares_h[t.half][:], veps_h[:], rstd_h[:], eps_h_done, rstd_h_done, g + 1)
                        wait(pool, rstd_h_done, g + 1, passed)
                        nc.gpsimd.tensor_tensor(gate[:], rows[t.half][:, :, D:DG],
                                                rstd_h[:].unsqueeze(2).broadcast_to([128, GT, E]),
                                                ALU.mult).then_inc(gate_step, 1)
                        wait(pool, gate_step, g + 1, passed)
                        wait(pool, chosen_done, g, passed)
                        nc.gpsimd.tensor_tensor(gate_b[:], gate[:], c["gbias"][:].unsqueeze(1).broadcast_to([128, GT, E]),
                                                ALU.add).then_inc(gate_done, 1)

                nc.gpsimd.memset(pad[:, :, 0:DG], 0.0).then_inc(pad_set, 1)
                nc.gpsimd.memset(pad[:, :, DG:ROW], float(NO_TOKEN)).then_inc(pad_set, 1)
                nc.gpsimd.iota(limit[:], pattern=[[TILE, LEAST_TILES]], base=0, channel_multiplier=0,
                               allow_small_or_imprecise_dtypes=True).then_inc(iota_set, 1)
                nc.gpsimd.iota(index[:], pattern=[[1, TILES]], base=0, channel_multiplier=0,
                               allow_small_or_imprecise_dtypes=True).then_inc(iota_set, 1)
                nc.gpsimd.iota(region[:], pattern=[[REGION, E]], base=0, channel_multiplier=0,
                               allow_small_or_imprecise_dtypes=True).then_inc(iota_set, 1)
                pool.wait_ge(iota_set, 3)
                nc.gpsimd.memset(neg_half[:], -0.5).then_inc(constants, 1)
                for e in range(E):
                    nc.gpsimd.memset(order[:, :, e:e + 1], float(E - e)).then_inc(constants, 1)
                nc.gpsimd.tensor_copy(number[:], c["number"][:]).then_inc(number_next, 1)
                pool.wait_ge(constants, 1 + E)
                loop(pool, step)
                for u in range(STEPS):
                    pool.wait_ge(scattered[u], 16 * (GROUPS // 2))


def first_row_of(sp, c, j):
    return sp.value_load(c["row_i"][0:1, bass.ds(j, 1)], min_val=0, max_val=ALL_ROWS - TILE)


def expert_of(sp, c, j):
    return sp.value_load(c["expert_i"][0:1, bass.ds(j, 1)], min_val=0, max_val=E - 1)


def load_w1(sp, c, a, u, expert):
    sp.dma_start(c["w1"][u][:], a["w1"][bass.ds(expert, 1)].rearrange("o (k p) f -> p (o k) f", k=ND))\
        .then_inc(c["w_loaded"][u], 16)


def load_w2(sp, c, a, u, expert):
    one = bass.ds(expert, 1)
    for dst, src in ((c["w2"][u][:], a["w2"][one].rearrange("o (k p) f -> p (o k) f", k=KH)),
                     (c["b1"][u][:], a["b1T"][one].rearrange("o p k -> (o p) k")),
                     (c["b2"][u][:], a["b2"][one].rearrange("o d -> (o d)").partition_broadcast(128))):
        sp.dma_start(dst, src).then_inc(c["w_loaded"][u], 16)


def experts(nc, sem, c, a, dram, out, passed):
    with ExitStack() as ctx:
        def sb(name, shape, dt=F32):
            return ctx.enter_context(nc.sbuf_tensor("experts_" + name, shape, dt))

        def ps(name, p=128):
            return ctx.enter_context(nc.psum_tensor("experts_" + name, [p, 512], F32))

        x_in = [sb(f"x_in{u}", [128, SLOTS, ROW]) for u in range(2)]
        w1, w2, b1, b2, w_loaded = c["w1"], c["w2"], c["b1"], c["b2"], c["w_loaded"]
        h1b2 = [sb(f"h1b2_{u}", [128, SLOTS, D]) for u in range(2)]
        token = [sb(f"token{u}", [128, SLOTS], I32) for u in range(2)]
        stats = sb("stats_e", [128, SLOTS, 6])
        mv = sb("mv_e", [128, SLOTS, 2])
        veps = sb("veps_e", [128, SLOTS])
        rstd = sb("rstd_e", [128, SLOTS])
        neg_half = sb("neg_half_e", [128, 1])
        xn = [sb(f"xn_e{u}", [128, SLOTS, D]) for u in range(2)]
        xn_part = [[sb(f"xn_part{part}_{u}", [KD, ND, TILE], F32R) for part in range(2)] for u in range(2)]
        w1_part = [[sb(f"w1_part{part}_{u}", [KD, ND, HID], F32R) for part in range(2)] for u in range(2)]
        x_upper = sb("x_upper", [KD, ND, TILE])
        w1_upper = sb("w1_upper", [KD, ND, HID])
        hT = sb("hT", [128, KH, TILE])
        y_out = [sb(f"y_out{u}", [128, SLOTS, D]) for u in range(2)]
        p_t = [ps(f"p_te{k}", KD) for k in range(ND)]
        p_h = [ps(f"p_he{i}") for i in range(4)]
        p_o = [ps(f"p_oe{i}") for i in range(2)]

        x_loaded = [sem(f"e_x_loaded{u}") for u in range(2)]
        written = [sem(f"e_written{u}") for u in range(2)]
        names = ("stats_done", "mv_done", "eps_done",
                 "rstd_done", "xn_done", "t_done", "x_masked", "x_high", "x_low", "w_masked", "w_high", "w_low",
                 "up_done", "gelu_done",
                 "down_done", "y_done", "h1b2_done", "token_done", "half_set")
        (stats_done, mv_done, eps_done, rstd_done, xn_done, t_done,
         x_masked, x_high, x_low, w_masked, w_high, w_low,
         up_done, gelu_done, down_done, y_done, h1b2_done, token_done, half_set) = (sem("e_" + n) for n in names)
        XL, WL = 16, 16 * 4

        def loop(engine, step):
            for j in range(2):
                step(j, j)
            with engine.Fori(1, TILES // 2 - 1) as i:
                for u in range(2):
                    step(i * 2 + u, u)
            for j in range(TILES - 2, TILES):
                step(j, j % 2)

        def later(j, n=1):
            return not isinstance(j, int) or j + n < TILES

        def round_of(j, u, per):
            return (j - u) * (per // 2) + per

        with nc.Block() as block:
            @block.sync
            def _(sp):
                def load_rows(u, row):
                    sp.dma_start(x_in[u][:], dram["rows"][bass.ds(row, TILE), :].rearrange("(p i) d -> p i d", p=128))\
                        .then_inc(x_loaded[u], 16)

                for j in range(2):
                    load_rows(j, first_row_of(sp, c, j))
                with sp.Fori(0, TILES // 2 - 1) as i:
                    for u in range(2):
                        row, expert = first_row_of(sp, c, i * 2 + (2 + u)), expert_of(sp, c, i * 2 + (2 + u))
                        by_slot = sp.snap(i * (2 * SLOTS) + (1 + u) * SLOTS)
                        by_tile = sp.snap(i * 2 + (1 + u))
                        wait(sp, xn_done, by_slot, passed)
                        wait(sp, token_done, by_tile, passed)
                        load_rows(u, row)
                        wait(sp, w_low, by_tile, passed)
                        load_w1(sp, c, a, u, expert)
                        wait(sp, down_done, by_slot, passed)
                        load_w2(sp, c, a, u, expert)

            @block.gpsimd
            def _(pool):
                nc.gpsimd.memset(neg_half[:], -0.5).then_inc(half_set, 1)
                pool.wait_ge(half_set, 1)

                def normal(j, u):
                    wait(pool, mv_done, SLOTS * (j + 1), passed)
                    wait(pool, xn_done, SLOTS * j, passed)
                    nc.gpsimd.tensor_scalar(veps[:], mv[:, :, 1], EPS, None, ALU.add).then_inc(eps_done, 1)
                    wait(pool, eps_done, j + 1, passed)
                    nc.gpsimd.tensor_tensor(rstd[:], veps[:], neg_half[:].broadcast_to([128, SLOTS]),
                                            ALU.pow).then_inc(rstd_done, 1)
                    pool.wait_ge(w_loaded[u], round_of(j, u, WL))
                    if not (isinstance(j, int) and j < 2):
                        wait(pool, written[u], (j - u) * (8 * SLOTS), passed)
                    nc.gpsimd.tensor_tensor(h1b2[u][:], x_in[u][:, :, 0:D],
                                            b2[u][:].unsqueeze(1).broadcast_to([128, SLOTS, D]),
                                            ALU.add).then_inc(h1b2_done, 1)
                    nc.gpsimd.tensor_copy(token[u][:], x_in[u][:, :, DG]).then_inc(token_done, 1)

                def step(j, u):
                    if later(j):
                        normal(j + 1, 1 - u)
                    wait(pool, token_done, j + 1, passed)
                    for i in range(SLOTS):
                        wait(pool, y_done, SLOTS * j + i + 1, passed)
                        nc.gpsimd.indirect_dma_start(out, bass.IndirectOffsetOnAxis(ap=token[u][:, i:i + 1], axis=0),
                                                     y_out[u][:, i, :], None, bounds_check=N - 1,
                                                     oob_is_err=False).then_inc(written[u], 16)

                normal(0, 0)
                loop(pool, step)
                for u in range(2):
                    pool.wait_ge(written[u], 16 * SLOTS * (TILES // 2))

            @block.vector
            def _(dve):
                def normal(j, u):
                    wait(dve, x_loaded[u], round_of(j, u, XL))
                    for i in range(SLOTS):
                        nc.vector.bn_stats(stats[:, i, :], x_in[u][:, i, 0:D]).then_inc(stats_done, 1)
                    wait(dve, eps_done, j)
                    wait(dve, stats_done, SLOTS * (j + 1), passed)
                    for i in range(SLOTS):
                        nc.vector.bn_aggr(mv[:, i, :], stats[:, i, :]).then_inc(mv_done, 1)
                    dve.wait_ge(rstd_done, j + 1)
                    for i in range(SLOTS):
                        nc.vector.tensor_scalar(xn[u][:, i, :], x_in[u][:, i, 0:D], mv[:, i, 0:1], rstd[:, i:i + 1],
                                                ALU.subtract, ALU.mult).then_inc(xn_done, 1)

                def split(j, u):
                    wait(dve, w_loaded[u], round_of(j, u, WL))
                    wait(dve, w_high, j)
                    nc.vector.tensor_scalar(w1_upper[:].bitcast(I32), w1[u][:].bitcast(I32), UPPER, None,
                                            ALU.bitwise_and).then_inc(w_masked, 1)
                    dve.wait_ge(w_masked, j + 1)
                    nc.vector.tensor_tensor(w1_part[u][1][:], w1[u][:], w1_upper[:], ALU.subtract).then_inc(w_low, 1)
                    wait(dve, x_high, j)
                    for k in range(ND):
                        dve.wait_ge(t_done, ND * j + k + 1)
                        nc.vector.tensor_scalar(x_upper[:, k, :].bitcast(I32), p_t[k][:, 0:TILE].bitcast(I32), UPPER, None,
                                                ALU.bitwise_and).then_inc(x_masked, 1)
                    for k in range(ND):
                        dve.wait_ge(x_masked, ND * j + k + 1)
                        nc.vector.tensor_tensor(xn_part[u][1][:, k, :], p_t[k][:, 0:TILE], x_upper[:, k, :],
                                                ALU.subtract).then_inc(x_low, 1)

                def step(j, u):
                    if later(j):
                        normal(j + 1, 1 - u)
                        split(j + 1, 1 - u)
                    dve.wait_ge(h1b2_done, j + 1)
                    if not (isinstance(j, int) and j < 2):
                        dve.wait_ge(written[u], (j - u) * (8 * SLOTS))
                    for i in range(SLOTS):
                        dve.wait_ge(down_done, SLOTS * j + i + 1)
                        nc.vector.tensor_tensor(y_out[u][:, i, :], p_o[(SLOTS * u + i) % 2][:, 0:D], h1b2[u][:, i, :],
                                                ALU.add).then_inc(y_done, 1)

                normal(0, 0)
                split(0, 0)
                loop(dve, step)

            @block.scalar
            def _(act):
                def copy_upper(j, u):
                    act.wait_ge(w_masked, j + 1)
                    nc.scalar.copy(w1_part[u][0][:], w1_upper[:]).then_inc(w_high, 1)
                    act.wait_ge(x_masked, ND * (j + 1))
                    nc.scalar.copy(xn_part[u][0][:], x_upper[:]).then_inc(x_high, 1)

                def step(j, u):
                    for m in range(KH):
                        act.wait_ge(up_done, KH * j + m + 1)
                        if m == 0:
                            act.wait_ge(w_loaded[u], round_of(j, u, WL))
                        nc.scalar.activation(hT[:, m, :], p_h[(KH * u + m) % 4][:, 0:TILE], ACT.Gelu,
                                             bias=b1[u][:, m:m + 1]).then_inc(gelu_done, 1)
                    if later(j):
                        copy_upper(j + 1, 1 - u)

                copy_upper(0, 0)
                loop(act, step)

            @block.tensor
            def _(pe):
                def transposes(j, u):
                    pe.wait_ge(xn_done, SLOTS * (j + 1))
                    wait(pe, x_low, ND * j)
                    for k in range(ND):
                        for i in range(SLOTS):
                            mm = nc.tensor.transpose(p_t[k][:, i * 128:(i + 1) * 128], xn[u][:, i, k * KD:(k + 1) * KD],
                                                     c["ident"][:])
                        mm.then_inc(t_done, 1)

                def step(j, u):
                    pe.wait_ge(w_loaded[u], round_of(j, u, WL))
                    pe.wait_ge(w_low, j + 1)
                    pe.wait_ge(w_high, j + 1)
                    pe.wait_ge(x_high, j + 1)
                    pe.wait_ge(x_low, ND * (j + 1))
                    for m in range(KH):
                        wait(pe, gelu_done, KH * j + m - 3)
                        jobs = [(k, wp, xp) for k in range(ND) for wp, xp in HIGH_LOW]
                        for n, (k, wp, xp) in enumerate(jobs):
                            mm = nc.tensor.matmul(p_h[(KH * u + m) % 4][:, 0:TILE],
                                                  w1_part[u][wp][:, k, m * 128:(m + 1) * 128], xn_part[u][xp][:, k, :],
                                                  start=n == 0, stop=n == len(jobs) - 1)
                        mm.then_inc(up_done, 1)
                    if later(j):
                        transposes(j + 1, 1 - u)
                    pe.wait_ge(gelu_done, KH * j + KH - 2)
                    for i in range(SLOTS):
                        wait(pe, y_done, SLOTS * j + i - 1)
                        for k in range(KH):
                            if i == 0 and k == KH - 2:
                                pe.wait_ge(gelu_done, KH * (j + 1))
                            mm = nc.tensor.matmul(p_o[(SLOTS * u + i) % 2][:, 0:D], hT[:, k, i * 128:(i + 1) * 128],
                                                  w2[u][:, k, :], start=k == 0, stop=k == KH - 1)
                        mm.then_inc(down_done, 1)

                transposes(0, 0)
                loop(pe, step)


def build(nc, a, out):
    dram = {"rows": nc.dram_tensor("rows", [ALL_ROWS, ROW], F32, kind="Internal").ap()}
    with ExitStack() as ctx:
        def sb(name, shape, dt=F32):
            return ctx.enter_context(nc.sbuf_tensor(name, shape, dt))

        def in_phase(stack):
            return lambda name: stack.enter_context(nc.semaphore(name))

        c = {
            "ident": sb("ident", [128, 128]),
            "before": sb("before", [128, 128], BF16),
            "ones_b": sb("ones_b", [128, 128], BF16),
            "number": sb("number", [128, GT]),
            "next_row": sb("next_row", [128, E]),
            "WT": sb("WT", [128, KI, DG]),
            "bias": sb("bias", [128, DG]),
            "WqkvT": sb("WqkvT", [KD, ND, 3 * D]),
            "WoT": sb("WoT", [KD, ND, DG]),
            "neg_lambda": sb("neg_lambda", [128, 1]),
            "gbias": sb("gbias_c", [128, E]),
            "x_sb": [sb(f"x_sb{i}", [128, KI, GTOK]) for i in range(2)],
            "x_loaded": [ctx.enter_context(nc.semaphore(f"x_loaded{i}")) for i in range(2)],
            "expert_i": sb("expert_i", [1, TILES], I32),
            "row_i": sb("row_i", [1, TILES], I32),
            "fill_i": sb("fill_i", [1, E], I32),
            "w1": [sb(f"w1_{u}", [KD, ND, HID]) for u in range(2)],
            "w2": [sb(f"w2_{u}", [128, KH, D]) for u in range(2)],
            "b1": [sb(f"b1_{u}", [128, KH]) for u in range(2)],
            "b2": [sb(f"b2_{u}", [128, D]) for u in range(2)],
            "w_loaded": [ctx.enter_context(nc.semaphore(f"w_loaded{u}")) for u in range(2)],
        }
        passed = ctx.enter_context(nc.semaphore("passed"))
        for phase in (lambda sem: prepare(nc, sem, c, a, passed), lambda sem: attend(nc, sem, c, a, dram, passed),
                      lambda sem: experts(nc, sem, c, a, dram, out, passed)):
            with ExitStack() as stack:
                phase(in_phase(stack))


def kernel(x, L0_tok_W, L0_tok_b, L0_attn_W_attn, L0_attn_W_out, L0_attn_lambda_q1, L0_attn_lambda_k1,
           L0_attn_lambda_q2, L0_attn_lambda_k2, L0_ffn_gate_w, L0_ffn_gate_b, L0_ffn_gate_center, L0_ffn_w1,
           L0_ffn_b1, L0_ffn_w2, L0_ffn_b2):
    import numpy as np
    import concourse.bacc as bacc
    from concourse.bass_utils import run_bass_kernel_spmd as run

    nc = bacc.Bacc("TRN2", target_bir_lowering=False, num_devices=1)
    x = np.asarray(x)
    patches = x.reshape(IMAGES, CHANNELS, SIDE, PATCH, SIDE, PATCH).transpose(1, 3, 5, 0, 2, 4)
    arrays = {
        "xT": patches.reshape(KI, 128, N),
        "tok_W": np.asarray(L0_tok_W), "tok_WT": np.asarray(L0_tok_W).T,
        "tok_b": np.asarray(L0_tok_b), "tok_b_col": np.asarray(L0_tok_b).reshape(ND, KD).T,
        "W_attnT": np.asarray(L0_attn_W_attn).T,
        "W_out": np.asarray(L0_attn_W_out), "W_outT": np.asarray(L0_attn_W_out).T,
        "lambda_q1": np.asarray(L0_attn_lambda_q1), "lambda_k1": np.asarray(L0_attn_lambda_k1),
        "lambda_q2": np.asarray(L0_attn_lambda_q2), "lambda_k2": np.asarray(L0_attn_lambda_k2),
        "gate_w": np.asarray(L0_ffn_gate_w), "gate_b": np.asarray(L0_ffn_gate_b),
        "gate_center": np.asarray(L0_ffn_gate_center),
        "w1": np.asarray(L0_ffn_w1), "w2": np.asarray(L0_ffn_w2),
        "b1T": np.asarray(L0_ffn_b1).reshape(E, KH, 128).transpose(0, 2, 1), "b2": np.asarray(L0_ffn_b2),
    }
    arrays = {k: np.ascontiguousarray(v) for k, v in arrays.items()}
    a = {k: nc.dram_tensor(k, list(v.shape), mybir.dt.from_np(v.dtype), kind="ExternalInput").ap()
         for k, v in arrays.items()}
    out = nc.dram_tensor("out", [N, D], F32, kind="ExternalOutput").ap()
    build(nc, a, out)
    r = run(nc, [arrays], core_ids=[0])
    return r.results[0]["out"].reshape(IMAGES, TOK, D)
```
